# Optimizing a Trainium2 kernel written in Bass

```python
import numpy as np
import jax
import jax.numpy as jnp

def _softmax(x, axis=-1):
    return jax.nn.softmax(x, axis=axis)

def _gelu(x):
    return jax.nn.gelu(x, approximate=True)

def _silu(x):
    return jax.nn.silu(x)

def _sigmoid(x):
    return jax.nn.sigmoid(x)

def _layernorm(x, axis=-1, eps=1e-05):
    m = jnp.mean(x, axis=axis, keepdims=True)
    v = jnp.var(x, axis=axis, keepdims=True)
    return (x - m) / jnp.sqrt(v + eps)

def _scatter_add(tgt, idx, src, axis=0):
    return tgt.at[idx].add(src)

def _segment_sum(src, seg, n):
    return jax.ops.segment_sum(src, seg, n)
kernel_name = 'mk_gps_d2_gnn_r16_1bb50b'

def setup_inputs(seed: int=0):
    np.random.seed(seed)
    _w = jnp.asarray

    def _rec_inputs():
        import jax
        import jax.numpy as jnp
        _gk = jax.random.key(seed)
        x = -0.0003713 + 1 * jax.random.normal(jax.random.fold_in(_gk, 1), (3125, 256), jnp.float32)
        src = jax.random.randint(jax.random.fold_in(_gk, 2), (100000,), 0, 3125, jnp.int32)
        dst = jax.random.randint(jax.random.fold_in(_gk, 3), (100000,), 0, 3125, jnp.int32)
        _o = jnp.argsort(dst, stable=True)
        src = src[_o]
        dst = dst[_o]
        return (x, src, dst)
    x, src, dst = _rec_inputs()

    def _L0_gnn_setup():
        import jax, jax.numpy as jnp
        import numpy as np
        N_NODES = 3125
        N_EDGES = 50000
        IN_FEAT = 256
        HEADS = 4
        OUT_FEAT = 64
        NEG_SLOPE = 0.2
        key = jax.random.key(seed)
        k1, k2, k3, k4, k5, k6 = jax.random.split(key, 6)
        x = jax.random.normal(k1, (N_NODES, IN_FEAT), dtype=jnp.float32)
        edge_index = jax.random.randint(k2, (2, N_EDGES), 0, N_NODES, dtype=jnp.int64)
        scale = 1.0 / np.sqrt(IN_FEAT)
        W = jax.random.normal(k3, (IN_FEAT, HEADS * OUT_FEAT), dtype=jnp.float32) * scale
        att_src = jax.random.normal(k4, (HEADS, OUT_FEAT), dtype=jnp.float32) * scale
        att_dst = jax.random.normal(k5, (HEADS, OUT_FEAT), dtype=jnp.float32) * scale
        bias = jax.random.normal(k6, (HEADS * OUT_FEAT,), dtype=jnp.float32) * 0.01
        return {'x': x, 'edge_index': edge_index, 'W': W, 'att_src': att_src, 'att_dst': att_dst, 'bias': bias}
    _L0_gnn_all = _L0_gnn_setup()
    _L0_gnn_in = {k: v for k, v in _L0_gnn_all.items() if k in ('W', 'att_src', 'att_dst', 'bias')}
    del _L0_gnn_all

    def _L0_mix_setup():
        import jax, jax.numpy as jnp
        import numpy as np
        B, N, C = (8, 512, 256)
        HEADS, DH, KR = (8, 32, 4)
        INNER = HEADS * DH
        FF = 4 * C
        EPS = 1e-05

        def layernorm(x, g, b):
            mu = jnp.mean(x, axis=-1, keepdims=True)
            var = jnp.mean((x - mu) ** 2, axis=-1, keepdims=True)
            return (x - mu) * jax.lax.rsqrt(var + EPS) * g + b
        key = jax.random.key(seed)
        ks = jax.random.split(key, 16)
        s = 0.02
        return {'x': jax.random.normal(ks[0], (B, N, C), jnp.float32), 'ln1_g': jnp.ones((C,), jnp.float32), 'ln1_b': jnp.zeros((C,), jnp.float32), 'Wx': jax.random.normal(ks[1], (C, INNER), jnp.float32) * s, 'bx': jnp.zeros((INNER,), jnp.float32), 'Wq': jax.random.normal(ks[2], (DH, KR), jnp.float32) * s, 'Wk': jax.random.normal(ks[3], (DH, KR), jnp.float32) * s, 'Wv': jax.random.normal(ks[4], (DH, DH), jnp.float32) * s, 'Wo': jax.random.normal(ks[5], (INNER, C), jnp.float32) * s, 'bo': jnp.zeros((C,), jnp.float32), 'ln2_g': jnp.ones((C,), jnp.float32), 'ln2_b': jnp.zeros((C,), jnp.float32), 'W1': jax.random.normal(ks[6], (C, FF), jnp.float32) * s, 'b1': jnp.zeros((FF,), jnp.float32), 'W2': jax.random.normal(ks[7], (FF, C), jnp.float32) * s, 'b2': jnp.zeros((C,), jnp.float32)}
    _L0_mix_all = _L0_mix_setup()
    _L0_mix_in = {k: v for k, v in _L0_mix_all.items() if k in ('ln1_g', 'ln1_b', 'Wx', 'bx', 'Wq', 'Wk', 'Wv', 'Wo', 'bo', 'ln2_g', 'ln2_b', 'W1', 'b1', 'W2', 'b2')}
    del _L0_mix_all

    def _L0_ffn_setup():
        import jax, jax.numpy as jnp
        import numpy as np
        TOP_K = 2
        LN_EPS = 1e-05
        key = jax.random.key(seed)
        ks = jax.random.split(key, 8)
        B, S, D, E, H = (16, 1024, 256, 8, 1024)
        x = jax.random.normal(ks[0], (B, S, D), dtype=jnp.float32)
        Wr = jax.random.normal(ks[1], (D, E), dtype=jnp.float32) * 0.1
        br = jnp.zeros((E,), dtype=jnp.float32)
        ln_g = jnp.ones((E, D), dtype=jnp.float32)
        ln_b = jnp.zeros((E, D), dtype=jnp.float32)
        W1 = jax.random.normal(ks[2], (E, D, H), dtype=jnp.float32) * (1.0 / np.sqrt(D))
        b1 = jnp.zeros((E, H), dtype=jnp.float32)
        W2 = jax.random.normal(ks[3], (E, H, D), dtype=jnp.float32) * (1.0 / np.sqrt(H))
        b2 = jnp.zeros((E, D), dtype=jnp.float32)
        return {'x': x, 'Wr': Wr, 'br': br, 'ln_g': ln_g, 'ln_b': ln_b, 'W1': W1, 'b1': b1, 'W2': W2, 'b2': b2}
    _L0_ffn_all = _L0_ffn_setup()
    _L0_ffn_in = {k: v for k, v in _L0_ffn_all.items() if k in ('Wr', 'br', 'ln_g', 'ln_b', 'W1', 'b1', 'W2', 'b2')}
    del _L0_ffn_all

    def _L1_gnn_setup():
        import jax, jax.numpy as jnp
        import numpy as np
        N, E = (3125, 50000)
        IN, HID, OUT, HEADS = (256, 128, 256, 4)
        CAT = HEADS * HID

        def _gat(x, ei_src, ei_dst, W, a_src, a_dst, b, heads, out_ch, concat):
            n = x.shape[0]
            loop = jnp.arange(n, dtype=ei_src.dtype)
            src = jnp.concatenate([ei_src, loop])
            dst = jnp.concatenate([ei_dst, loop])
            h = (x @ W).reshape(n, heads, out_ch)
            al_s = jnp.einsum('nhc,hc->nh', h, a_src)
            al_d = jnp.einsum('nhc,hc->nh', h, a_dst)
            e = jax.nn.leaky_relu(al_s[src] + al_d[dst], 0.2)
            emax = jax.ops.segment_max(e, dst, num_segments=n)
            ee = jnp.exp(e - emax[dst])
            denom = jax.ops.segment_sum(ee, dst, num_segments=n)
            alpha = ee / (denom[dst] + 1e-16)
            out = jax.ops.segment_sum(h[src] * alpha[:, :, None], dst, num_segments=n)
            out = out.reshape(n, heads * out_ch) if concat else out.mean(axis=1)
            return out + b
        key = jax.random.key(seed)
        ks = jax.random.split(key, 20)
        g = lambda k, shape, fan: (jax.random.normal(k, shape, jnp.float32) / np.sqrt(fan)).astype(jnp.float32)
        return {'x': jax.random.normal(ks[0], (N, IN), jnp.float32), 'edge_index': jax.random.randint(ks[1], (2, E), 0, N, dtype=jnp.int32), 'W1': g(ks[2], (IN, CAT), IN), 'a_src1': g(ks[3], (HEADS, HID), HID), 'a_dst1': g(ks[4], (HEADS, HID), HID), 'b1': jnp.zeros((CAT,), jnp.float32), 'W2': g(ks[5], (CAT, CAT), CAT), 'a_src2': g(ks[6], (HEADS, HID), HID), 'a_dst2': g(ks[7], (HEADS, HID), HID), 'b2': jnp.zeros((CAT,), jnp.float32), 'W3': g(ks[8], (CAT, OUT), CAT), 'a_src3': g(ks[9], (1, OUT), OUT), 'a_dst3': g(ks[10], (1, OUT), OUT), 'b3': jnp.zeros((OUT,), jnp.float32), 'M1': g(ks[11], (OUT, 2 * HID), OUT), 'mb1': jnp.zeros((2 * HID,), jnp.float32), 'M2': g(ks[12], (2 * HID, HID), 2 * HID), 'mb2': jnp.zeros((HID,), jnp.float32), 'M3': g(ks[13], (HID, OUT), HID), 'mb3': jnp.zeros((OUT,), jnp.float32)}
    _L1_gnn_all = _L1_gnn_setup()
    _L1_gnn_in = {k: v for k, v in _L1_gnn_all.items() if k in ('W1', 'a_src1', 'a_dst1', 'b1', 'W2', 'a_src2', 'a_dst2', 'b2', 'W3', 'a_src3', 'a_dst3', 'b3', 'M1', 'mb1', 'M2', 'mb2', 'M3', 'mb3')}
    del _L1_gnn_all

    def _L1_mix_setup():
        import jax, jax.numpy as jnp
        import numpy as np
        HEADS, DIM_HEAD = (8, 64)
        EPS = 1e-05

        def instance_norm(t):
            mu = jnp.mean(t, axis=-1, keepdims=True)
            var = jnp.mean((t - mu) ** 2, axis=-1, keepdims=True)
            return (t - mu) * jax.lax.rsqrt(var + EPS)
        key = jax.random.key(seed)
        k1, k2, k3, k4 = jax.random.split(key, 4)
        B, N, D = (8, 512, 256)
        inner = HEADS * DIM_HEAD
        x = jax.random.normal(k1, (B, N, D), jnp.float32)
        w_qkv = jax.random.normal(k2, (3 * inner, D), jnp.float32) / np.sqrt(D).astype(np.float32)
        w_out = jax.random.normal(k3, (D, inner), jnp.float32) / np.sqrt(inner).astype(np.float32)
        b_out = 0.01 * jax.random.normal(k4, (D,), jnp.float32)
        return {'x': x, 'w_qkv': w_qkv, 'w_out': w_out, 'b_out': b_out}
    _L1_mix_all = _L1_mix_setup()
    _L1_mix_in = {k: v for k, v in _L1_mix_all.items() if k in ('w_qkv', 'w_out', 'b_out')}
    del _L1_mix_all

    def _L1_ffn_setup():
        import jax, jax.numpy as jnp
        import numpy as np
        B, A = (256, 8)
        IN, OUT = (256, 256)
        SH1, SH2 = (256, 128)
        EH1, EH2 = (128, 64)
        E, TOPK = (4, 2)

        def _shared_mlp(x, W1, b1, W2, b2, W3, b3):
            h = jax.nn.relu(x @ W1 + b1)
            h = jax.nn.relu(h @ W2 + b2)
            return h @ W3 + b3

        def _experts_mlp(x, eW1, eb1, eW2, eb2, eW3, eb3):
            h = jax.nn.relu(jnp.einsum('baf,efh->ebah', x, eW1) + eb1[:, None, None, :])
            h = jax.nn.relu(jnp.einsum('ebah,ehg->ebag', h, eW2) + eb2[:, None, None, :])
            o = jnp.einsum('ebag,ego->ebao', h, eW3) + eb3[:, None, None, :]
            return jnp.moveaxis(o, 0, -1)
        key = jax.random.key(seed)
        ks = jax.random.split(key, 16)
        s = 0.05
        return {'x': jax.random.normal(ks[0], (B, A, IN), jnp.float32), 'sW1': jax.random.normal(ks[1], (IN, SH1), jnp.float32) * s, 'sb1': jnp.zeros((SH1,), jnp.float32), 'sW2': jax.random.normal(ks[2], (SH1, SH2), jnp.float32) * s, 'sb2': jnp.zeros((SH2,), jnp.float32), 'sW3': jax.random.normal(ks[3], (SH2, OUT), jnp.float32) * s, 'sb3': jnp.zeros((OUT,), jnp.float32), 'eW1': jax.random.normal(ks[4], (E, IN, EH1), jnp.float32) * s, 'eb1': jnp.zeros((E, EH1), jnp.float32), 'eW2': jax.random.normal(ks[5], (E, EH1, EH2), jnp.float32) * s, 'eb2': jnp.zeros((E, EH2), jnp.float32), 'eW3': jax.random.normal(ks[6], (E, EH2, OUT), jnp.float32) * s, 'eb3': jnp.zeros((E, OUT), jnp.float32), 'gW': jax.random.normal(ks[7], (IN, E), jnp.float32) * s, 'gb': jnp.zeros((E,), jnp.float32)}
    _L1_ffn_all = _L1_ffn_setup()
    _L1_ffn_in = {k: v for k, v in _L1_ffn_all.items() if k in ('sW1', 'sb1', 'sW2', 'sb2', 'sW3', 'sb3', 'eW1', 'eb1', 'eW2', 'eb2', 'eW3', 'eb3', 'gW', 'gb')}
    del _L1_ffn_all
    return {'x': x, 'src': src, 'dst': dst, 'L0_gnn_W': _L0_gnn_in['W'], 'L0_gnn_att_src': _L0_gnn_in['att_src'], 'L0_gnn_att_dst': _L0_gnn_in['att_dst'], 'L0_gnn_bias': _L0_gnn_in['bias'], 'L0_mix_ln1_g': _L0_mix_in['ln1_g'], 'L0_mix_ln1_b': _L0_mix_in['ln1_b'], 'L0_mix_Wx': _L0_mix_in['Wx'], 'L0_mix_bx': _L0_mix_in['bx'], 'L0_mix_Wq': _L0_mix_in['Wq'], 'L0_mix_Wk': _L0_mix_in['Wk'], 'L0_mix_Wv': _L0_mix_in['Wv'], 'L0_mix_Wo': _L0_mix_in['Wo'], 'L0_mix_bo': _L0_mix_in['bo'], 'L0_mix_ln2_g': _L0_mix_in['ln2_g'], 'L0_mix_ln2_b': _L0_mix_in['ln2_b'], 'L0_mix_W1': _L0_mix_in['W1'], 'L0_mix_b1': _L0_mix_in['b1'], 'L0_mix_W2': _L0_mix_in['W2'], 'L0_mix_b2': _L0_mix_in['b2'], 'L0_ffn_Wr': _L0_ffn_in['Wr'], 'L0_ffn_br': _L0_ffn_in['br'], 'L0_ffn_ln_g': _L0_ffn_in['ln_g'], 'L0_ffn_ln_b': _L0_ffn_in['ln_b'], 'L0_ffn_W1': _L0_ffn_in['W1'], 'L0_ffn_b1': _L0_ffn_in['b1'], 'L0_ffn_W2': _L0_ffn_in['W2'], 'L0_ffn_b2': _L0_ffn_in['b2'], 'L1_gnn_W1': _L1_gnn_in['W1'], 'L1_gnn_a_src1': _L1_gnn_in['a_src1'], 'L1_gnn_a_dst1': _L1_gnn_in['a_dst1'], 'L1_gnn_b1': _L1_gnn_in['b1'], 'L1_gnn_W2': _L1_gnn_in['W2'], 'L1_gnn_a_src2': _L1_gnn_in['a_src2'], 'L1_gnn_a_dst2': _L1_gnn_in['a_dst2'], 'L1_gnn_b2': _L1_gnn_in['b2'], 'L1_gnn_W3': _L1_gnn_in['W3'], 'L1_gnn_a_src3': _L1_gnn_in['a_src3'], 'L1_gnn_a_dst3': _L1_gnn_in['a_dst3'], 'L1_gnn_b3': _L1_gnn_in['b3'], 'L1_gnn_M1': _L1_gnn_in['M1'], 'L1_gnn_mb1': _L1_gnn_in['mb1'], 'L1_gnn_M2': _L1_gnn_in['M2'], 'L1_gnn_mb2': _L1_gnn_in['mb2'], 'L1_gnn_M3': _L1_gnn_in['M3'], 'L1_gnn_mb3': _L1_gnn_in['mb3'], 'L1_mix_w_qkv': _L1_mix_in['w_qkv'], 'L1_mix_w_out': _L1_mix_in['w_out'], 'L1_mix_b_out': _L1_mix_in['b_out'], 'L1_ffn_sW1': _L1_ffn_in['sW1'], 'L1_ffn_sb1': _L1_ffn_in['sb1'], 'L1_ffn_sW2': _L1_ffn_in['sW2'], 'L1_ffn_sb2': _L1_ffn_in['sb2'], 'L1_ffn_sW3': _L1_ffn_in['sW3'], 'L1_ffn_sb3': _L1_ffn_in['sb3'], 'L1_ffn_eW1': _L1_ffn_in['eW1'], 'L1_ffn_eb1': _L1_ffn_in['eb1'], 'L1_ffn_eW2': _L1_ffn_in['eW2'], 'L1_ffn_eb2': _L1_ffn_in['eb2'], 'L1_ffn_eW3': _L1_ffn_in['eW3'], 'L1_ffn_eb3': _L1_ffn_in['eb3'], 'L1_ffn_gW': _L1_ffn_in['gW'], 'L1_ffn_gb': _L1_ffn_in['gb']}

def reference(x, src, dst, L0_gnn_W, L0_gnn_att_src, L0_gnn_att_dst, L0_gnn_bias, L0_mix_ln1_g, L0_mix_ln1_b, L0_mix_Wx, L0_mix_bx, L0_mix_Wq, L0_mix_Wk, L0_mix_Wv, L0_mix_Wo, L0_mix_bo, L0_mix_ln2_g, L0_mix_ln2_b, L0_mix_W1, L0_mix_b1, L0_mix_W2, L0_mix_b2, L0_ffn_Wr, L0_ffn_br, L0_ffn_ln_g, L0_ffn_ln_b, L0_ffn_W1, L0_ffn_b1, L0_ffn_W2, L0_ffn_b2, L1_gnn_W1, L1_gnn_a_src1, L1_gnn_a_dst1, L1_gnn_b1, L1_gnn_W2, L1_gnn_a_src2, L1_gnn_a_dst2, L1_gnn_b2, L1_gnn_W3, L1_gnn_a_src3, L1_gnn_a_dst3, L1_gnn_b3, L1_gnn_M1, L1_gnn_mb1, L1_gnn_M2, L1_gnn_mb2, L1_gnn_M3, L1_gnn_mb3, L1_mix_w_qkv, L1_mix_w_out, L1_mix_b_out, L1_ffn_sW1, L1_ffn_sb1, L1_ffn_sW2, L1_ffn_sb2, L1_ffn_sW3, L1_ffn_sb3, L1_ffn_eW1, L1_ffn_eb1, L1_ffn_eW2, L1_ffn_eb2, L1_ffn_eW3, L1_ffn_eb3, L1_ffn_gW, L1_ffn_gb):
    import jax
    import jax.numpy as jnp

    def _L0_gnn_ref(x, edge_index, W, att_src, att_dst, bias):
        import jax, jax.numpy as jnp
        import numpy as np
        N_NODES = 3125
        N_EDGES = 50000
        IN_FEAT = 256
        HEADS = 4
        OUT_FEAT = 64
        NEG_SLOPE = 0.2
        N = x.shape[0]
        H, C = att_src.shape
        h = (x @ W).reshape(N, H, C)
        a_src = jnp.sum(h * att_src[None], axis=-1)
        a_dst = jnp.sum(h * att_dst[None], axis=-1)
        loop = jnp.arange(N, dtype=edge_index.dtype)
        src = jnp.concatenate([edge_index[0], loop])
        dst = jnp.concatenate([edge_index[1], loop])
        alpha = jax.nn.leaky_relu(a_src[src] + a_dst[dst], NEG_SLOPE)
        m = jax.ops.segment_max(alpha, dst, num_segments=N)
        alpha = jnp.exp(alpha - jax.lax.stop_gradient(m)[dst])
        denom = jax.ops.segment_sum(alpha, dst, num_segments=N)
        alpha = alpha / (denom[dst] + 1e-16)
        msg = h[src] * alpha[:, :, None]
        out = jax.ops.segment_sum(msg, dst, num_segments=N)
        out = out.reshape(N, H * C) + bias
        return jax.nn.relu(out)

    def _L0_mix_ref(x, ln1_g, ln1_b, Wx, bx, Wq, Wk, Wv, Wo, bo, ln2_g, ln2_b, W1, b1, W2, b2):
        import jax, jax.numpy as jnp
        import numpy as np
        B, N, C = (8, 512, 256)
        HEADS, DH, KR = (8, 32, 4)
        INNER = HEADS * DH
        FF = 4 * C
        EPS = 1e-05

        def layernorm(x, g, b):
            mu = jnp.mean(x, axis=-1, keepdims=True)
            var = jnp.mean((x - mu) ** 2, axis=-1, keepdims=True)
            return (x - mu) * jax.lax.rsqrt(var + EPS) * g + b
        b, n, c = x.shape
        h = layernorm(x, ln1_g, ln1_b)
        xm = h @ Wx + bx
        xm = xm.reshape(b, n, HEADS, DH).transpose(0, 2, 1, 3)
        q = jax.nn.softmax(xm @ Wq, axis=-1)
        k = jax.nn.softmax(xm @ Wk, axis=-2)
        v = xm @ Wv
        kv = jnp.einsum('bhnr,bhnd->bhrd', k, v)
        qkv = jnp.einsum('bhnr,bhrd->bhnd', q, kv)
        attn = qkv.transpose(0, 2, 1, 3).reshape(b, n, INNER) @ Wo + bo
        fx = attn + x
        h2 = layernorm(fx, ln2_g, ln2_b)
        m = jax.nn.gelu(h2 @ W1 + b1, approximate=False) @ W2 + b2
        return m + fx

    def _L0_ffn_ref(x, Wr, br, ln_g, ln_b, W1, b1, W2, b2):
        import jax, jax.numpy as jnp
        import numpy as np
        TOP_K = 2
        LN_EPS = 1e-05
        B, S, D = x.shape
        N = B * S
        xt = x.reshape(N, D)
        logits = xt @ Wr + br
        probs = jax.nn.softmax(logits, axis=-1)
        top_p, top_idx = jax.lax.top_k(probs, TOP_K)
        weights = top_p / top_p.sum(axis=-1, keepdims=True)
        mu = xt.mean(axis=-1, keepdims=True)
        var = ((xt - mu) ** 2).mean(axis=-1, keepdims=True)
        xn = (xt - mu) * jax.lax.rsqrt(var + LN_EPS)
        xe = xn[None, :, :] * ln_g[:, None, :] + ln_b[:, None, :]
        h = jax.nn.gelu(jnp.einsum('end,edh->enh', xe, W1) + b1[:, None, :], approximate=False)
        y = jnp.einsum('enh,ehd->end', h, W2) + b2[:, None, :]
        y_tok = jnp.transpose(y, (1, 0, 2))
        sel = jnp.take_along_axis(y_tok, top_idx[:, :, None], axis=1)
        out = (weights[:, :, None] * sel).sum(axis=1)
        return out.reshape(B, S, D)

    def _L1_gnn_ref(x, edge_index, W1, a_src1, a_dst1, b1, W2, a_src2, a_dst2, b2, W3, a_src3, a_dst3, b3, M1, mb1, M2, mb2, M3, mb3):
        import jax, jax.numpy as jnp
        import numpy as np
        N, E = (3125, 50000)
        IN, HID, OUT, HEADS = (256, 128, 256, 4)
        CAT = HEADS * HID

        def _gat(x, ei_src, ei_dst, W, a_src, a_dst, b, heads, out_ch, concat):
            n = x.shape[0]
            loop = jnp.arange(n, dtype=ei_src.dtype)
            src = jnp.concatenate([ei_src, loop])
            dst = jnp.concatenate([ei_dst, loop])
            h = (x @ W).reshape(n, heads, out_ch)
            al_s = jnp.einsum('nhc,hc->nh', h, a_src)
            al_d = jnp.einsum('nhc,hc->nh', h, a_dst)
            e = jax.nn.leaky_relu(al_s[src] + al_d[dst], 0.2)
            emax = jax.ops.segment_max(e, dst, num_segments=n)
            ee = jnp.exp(e - emax[dst])
            denom = jax.ops.segment_sum(ee, dst, num_segments=n)
            alpha = ee / (denom[dst] + 1e-16)
            out = jax.ops.segment_sum(h[src] * alpha[:, :, None], dst, num_segments=n)
            out = out.reshape(n, heads * out_ch) if concat else out.mean(axis=1)
            return out + b
        src, dst = (edge_index[0], edge_index[1])
        h = _gat(x, src, dst, W1, a_src1, a_dst1, b1, HEADS, HID, True)
        h = jax.nn.elu(h)
        h = _gat(h, src, dst, W2, a_src2, a_dst2, b2, HEADS, HID, True)
        h = jax.nn.elu(h)
        h = _gat(h, src, dst, W3, a_src3, a_dst3, b3, 1, OUT, False)
        r = jax.nn.relu(h @ M1 + mb1)
        r = jax.nn.relu(r @ M2 + mb2)
        return r @ M3 + mb3

    def _L1_mix_ref(x, w_qkv, w_out, b_out):
        import jax, jax.numpy as jnp
        import numpy as np
        HEADS, DIM_HEAD = (8, 64)
        EPS = 1e-05

        def instance_norm(t):
            mu = jnp.mean(t, axis=-1, keepdims=True)
            var = jnp.mean((t - mu) ** 2, axis=-1, keepdims=True)
            return (t - mu) * jax.lax.rsqrt(var + EPS)
        B, N, _ = x.shape
        H, Dh = (HEADS, DIM_HEAD)
        qkv = jnp.einsum('bnd,ed->bne', x, w_qkv)
        q, k, v = jnp.split(qkv, 3, axis=-1)

        def to_heads(t):
            return t.reshape(B, N, H, Dh).transpose(0, 2, 1, 3)
        q, k, v = (to_heads(q), to_heads(k), to_heads(v))
        k = instance_norm(k)
        v = instance_norm(v)
        dots = jnp.einsum('bhnd,bhne->bhde', k, v)
        out = jnp.einsum('bhnd,bhde->bhne', q, dots) / N
        out = out.transpose(0, 2, 1, 3).reshape(B, N, H * Dh)
        return jnp.einsum('bne,de->bnd', out, w_out) + b_out

    def _L1_ffn_ref(x, sW1, sb1, sW2, sb2, sW3, sb3, eW1, eb1, eW2, eb2, eW3, eb3, gW, gb):
        import jax, jax.numpy as jnp
        import numpy as np
        B, A = (256, 8)
        IN, OUT = (256, 256)
        SH1, SH2 = (256, 128)
        EH1, EH2 = (128, 64)
        E, TOPK = (4, 2)

        def _shared_mlp(x, W1, b1, W2, b2, W3, b3):
            h = jax.nn.relu(x @ W1 + b1)
            h = jax.nn.relu(h @ W2 + b2)
            return h @ W3 + b3

        def _experts_mlp(x, eW1, eb1, eW2, eb2, eW3, eb3):
            h = jax.nn.relu(jnp.einsum('baf,efh->ebah', x, eW1) + eb1[:, None, None, :])
            h = jax.nn.relu(jnp.einsum('ebah,ehg->ebag', h, eW2) + eb2[:, None, None, :])
            o = jnp.einsum('ebag,ego->ebao', h, eW3) + eb3[:, None, None, :]
            return jnp.moveaxis(o, 0, -1)
        all_out = _experts_mlp(x, eW1, eb1, eW2, eb2, eW3, eb3)
        shared = _shared_mlp(x, sW1, sb1, sW2, sb2, sW3, sb3)
        gates = jax.nn.softmax(x @ gW + gb, axis=-1)
        topv, topi = jax.lax.top_k(gates, TOPK)
        topw = jax.nn.softmax(topv, axis=-1)
        sel = jnp.take_along_axis(all_out, topi[:, :, None, :], axis=-1)
        gated = jnp.sum(sel * topw[:, :, None, :], axis=-1)
        return shared + gated
    edge_index = jnp.stack([src, dst])
    xn = _layernorm(x, axis=-1)
    x = x + _L0_gnn_ref(xn, edge_index, L0_gnn_W, L0_gnn_att_src, L0_gnn_att_dst, L0_gnn_bias) + _L0_mix_ref(xn[None], L0_mix_ln1_g, L0_mix_ln1_b, L0_mix_Wx, L0_mix_bx, L0_mix_Wq, L0_mix_Wk, L0_mix_Wv, L0_mix_Wo, L0_mix_bo, L0_mix_ln2_g, L0_mix_ln2_b, L0_mix_W1, L0_mix_b1, L0_mix_W2, L0_mix_b2)[0]
    x = x + _L0_ffn_ref(_layernorm(x, axis=-1)[None], L0_ffn_Wr, L0_ffn_br, L0_ffn_ln_g, L0_ffn_ln_b, L0_ffn_W1, L0_ffn_b1, L0_ffn_W2, L0_ffn_b2)[0]
    xn = _layernorm(x, axis=-1)
    x = x + _L1_gnn_ref(xn, edge_index, L1_gnn_W1, L1_gnn_a_src1, L1_gnn_a_dst1, L1_gnn_b1, L1_gnn_W2, L1_gnn_a_src2, L1_gnn_a_dst2, L1_gnn_b2, L1_gnn_W3, L1_gnn_a_src3, L1_gnn_a_dst3, L1_gnn_b3, L1_gnn_M1, L1_gnn_mb1, L1_gnn_M2, L1_gnn_mb2, L1_gnn_M3, L1_gnn_mb3) + _L1_mix_ref(xn[None], L1_mix_w_qkv, L1_mix_w_out, L1_mix_b_out)[0]
    x = x + _L1_ffn_ref(_layernorm(x, axis=-1)[None], L1_ffn_sW1, L1_ffn_sb1, L1_ffn_sW2, L1_ffn_sb2, L1_ffn_sW3, L1_ffn_sb3, L1_ffn_eW1, L1_ffn_eb1, L1_ffn_eW2, L1_ffn_eb2, L1_ffn_eW3, L1_ffn_eb3, L1_ffn_gW, L1_ffn_gb)[0]
    return x

_drawn_inputs = setup_inputs


def setup_inputs(seed=0):
    import zlib

    import numpy as np

    out = dict(_drawn_inputs(seed))
    spreads = {'L0_mix_ln1_g': (1.0, 0.6),
     'L0_mix_ln1_b': (0.0, 0.8),
     'L0_mix_bx': (0.0, 0.8),
     'L0_mix_bo': (0.0, 0.428),
     'L0_mix_ln2_g': (1.0, 0.6),
     'L0_mix_ln2_b': (0.0, 2.0),
     'L0_mix_b1': (0.0, 0.8),
     'L0_mix_b2': (0.0, 0.45),
     'L0_ffn_br': (0.0, 0.349),
     'L0_ffn_ln_g': (1.0, 0.6),
     'L0_ffn_ln_b': (0.0, 0.976),
     'L0_ffn_b1': (0.0, 0.934),
     'L0_ffn_b2': (0.0, 0.647),
     'L1_gnn_b1': (0.0, 2.0),
     'L1_gnn_b2': (0.0, 1.923),
     'L1_gnn_b3': (0.0, 1.436),
     'L1_gnn_mb1': (0.0, 1.492),
     'L1_gnn_mb2': (0.0, 1.124),
     'L1_gnn_mb3': (0.0, 0.737),
     'L1_ffn_sb1': (0.0, 2.0),
     'L1_ffn_sb2': (0.0, 2.0),
     'L1_ffn_sb3': (0.0, 0.796),
     'L1_ffn_eb1': (0.0, 2.0),
     'L1_ffn_eb2': (0.0, 2.0),
     'L1_ffn_eb3': (0.0, 0.8),
     'L1_ffn_gb': (0.0, 2.0)}
    factors = {'L0_gnn_att_dst': 29.48,
     'L0_gnn_bias': 38.59,
     'L0_mix_Wx': 8.0,
     'L0_mix_Wq': 8.0,
     'L0_mix_Wk': 8.0,
     'L0_mix_Wv': 8.0,
     'L0_mix_Wo': 8.0,
     'L1_gnn_W1': 3.132,
     'L1_gnn_a_src1': 5.021,
     'L1_gnn_a_dst1': 42.384,
     'L1_gnn_a_src2': 8.0,
     'L1_gnn_a_dst2': 36.062,
     'L1_gnn_a_src3': 21.357,
     'L1_gnn_a_dst3': 64.0,
     'L1_mix_b_out': 60.277,
     'L1_ffn_eW1': 12.321,
     'L0_gnn_W': 3.263,
     'L0_gnn_att_src': 6.73,
     'L1_ffn_sW1': 4.679,
     'L1_ffn_sW2': 3.148,
     'L1_ffn_eW2': 3.548,
     'L1_ffn_gW': 4.096}
    for name, (base, spread) in spreads.items():
        noise = np.random.default_rng([zlib.crc32(name.encode()), seed]).standard_normal(out[name].shape)
        drawn = base * np.exp(spread * noise) if base else spread * noise
        out[name] = jnp.asarray(drawn.astype(out[name].dtype))
    for name, factor in factors.items():
        out[name] = (out[name] * factor).astype(out[name].dtype)
    return out
```

```python
from contextlib import ExitStack

import concourse.bass as bass
from concourse import mybir

ALU = mybir.AluOpType
ACT = mybir.ActivationFunctionType
AX_X = mybir.AxisListType.X
F32 = mybir.dt.float32
BF16 = mybir.dt.bfloat16
I32 = mybir.dt.int32
ds = bass.ds

N = 3125
R = 125
T = N // R
U = 5
D = 256
P = 128
CUT = 112
EPS = 1e-5
NEG = 1e30
ROUND = 12582912.0
RING3 = [0, 1, 0, 1, 2]


def uses(i, k):
    return i * RING3.count(RING3[k]) + RING3[:k].count(RING3[k])


class Stage:

    def __init__(self, nc, name):
        self.nc, self.name, self.ctx, self.sems = nc, name, ExitStack(), []

    def __enter__(self):
        self.tick = self.sem("tick")
        return self

    def sb(self, name, shape, dt=F32):
        return self.ctx.enter_context(self.nc.sbuf_tensor(f"{self.name}_{name}", shape, dt))

    def ps(self, name, banks):
        return self.ctx.enter_context(self.nc.psum_tensor(f"{self.name}_{name}", [P, banks, 512], F32))

    def sem(self, name):
        h = self.nc.alloc_semaphore(f"{self.name}_{name}")
        self.sems.append(h)
        return h

    def block(self):
        return self.ctx.enter_context(self.nc.Block())

    def __exit__(self, *exc):
        self.ctx.close()
        if exc[0] is None and self.sems:
            self.nc.clear_and_free_semaphores(self.sems)
            self.nc.all_engine_barrier()


def tile_dma(eng, dst, src, sem):
    eng.dma_start(dst[0:CUT], src[0:CUT]).then_inc(sem, 16)
    eng.dma_start(dst[CUT:R], src[CUT:R]).then_inc(sem, 16)


def wait_apart(eng, tick, sem, value):
    eng.wait_ge(sem, value)
    eng.sem_inc(tick, 1)


def cols(ap):
    return ap.rearrange("p o n -> p (o n)")




def floor_div(nc, out, x, n):
    nc.vector.tensor_scalar(out, x, 1.0 / n, 0.5 / n - 0.5, ALU.mult, ALU.add)
    nc.vector.drain()
    nc.vector.tensor_scalar(out, out, ROUND, None, ALU.add)
    nc.vector.drain()
    nc.vector.tensor_scalar(out, out, ROUND, None, ALU.subtract)
    nc.vector.drain()


W5 = 5
NW = N // W5
CAP = 256
ALIGN = 32
EDGES = 100000
EP = EDGES // R
QW = W5 * T


def stage_edge_codes(nc, m):
    HB = EP // 8
    with Stage(nc, "codes") as s:
        srci, dsti = s.sb("srci", [R, EP], I32), s.sb("dsti", [R, EP], I32)
        srcf, dstf = s.sb("srcf", [R, EP]), s.sb("dstf", [R, EP])
        hi, win = s.sb("hi", [R, EP]), s.sb("win", [R, EP])
        wu, wv = s.sb("wu", [R, EP]), s.sb("wv", [R, EP])
        qb = s.sb("qb", [R, EP, 2])
        pad = s.sb("pad", [P, 2, 2])
        ohu, ohv = s.sb("ohu", [R, 2, HB, 25], BF16), s.sb("ohv", [R, 2, HB, 25], BF16)
        hist, histT = s.sb("hist", [25, 25]), s.sb("histT", [25, 25])
        base, lo = s.sb("base", [25, 1]), s.sb("lo", [25, 25], I32)
        psh = s.ps("psh", 8)
        loaded, coded, stored = s.sem("loaded"), s.sem("coded"), s.sem("stored")
        hot, counted, summed, prefix = s.sem("hot"), s.sem("counted"), s.sem("summed"), s.sem("prefix")
        spent = s.sem("spent")
        block = s.block()

        @block.sync
        def _(sp):
            sp.dma_start(srci[:], m.src.rearrange("(p c) -> p c", p=R)).then_inc(loaded, 16)
            sp.dma_start(dsti[:], m.dst.rearrange("(p c) -> p c", p=R)).then_inc(loaded, 16)
            sp.wait_ge(coded, 1)
            sp.dma_start(m.QB[0:EDGES].rearrange("(p c) k -> p c k", p=R), qb[:]).then_inc(stored, 16)
            sp.dma_start(m.QB[EDGES:EDGES + CAP].rearrange("(p c) k -> p c k", p=P), pad[:]).then_inc(stored, 16)
            sp.wait_ge(summed, 3)
            sp.dma_start(m.LO, lo[:]).then_inc(stored, 16)
            sp.wait_ge(stored, 48)

        @block.vector
        def _(dve):
            nc.vector.memset(pad[:, :, 0:1], -1.0)
            nc.vector.memset(pad[:, :, 1:2], 0.0)
            dve.wait_ge(loaded, 32)
            nc.vector.tensor_copy(srcf[:], srci[:])
            nc.vector.tensor_copy(dstf[:], dsti[:])
            nc.vector.drain()
            floor_div(nc, hi[:], srcf[:], R)
            nc.vector.scalar_tensor_tensor(out=qb[:, :, 1], in0=hi[:], scalar=-float(R), in1=srcf[:], op0=ALU.mult, op1=ALU.add)
            nc.vector.scalar_tensor_tensor(out=qb[:, :, 0], in0=dstf[:], scalar=float(T), in1=hi[:], op0=ALU.mult, op1=ALU.add).then_inc(coded, 1)
            floor_div(nc, win[:], dstf[:], W5)
            floor_div(nc, wu[:], win[:], 25)
            nc.vector.scalar_tensor_tensor(out=wv[:], in0=wu[:], scalar=-25.0, in1=win[:], op0=ALU.mult, op1=ALU.add)
            nc.vector.drain()
            iota = m.iota[0:R, 0:25].unsqueeze(1).to_broadcast([R, HB, 25])
            spent_base = 0
            with dve.Fori(0, 4) as i:
                for par in range(2):
                    dve.wait_ge(spent, i * 2 + par + 1)
                    for oh, x in ((ohu, wu), (ohv, wv)):
                        code = x[:, ds((i * 2 + par) * HB, HB)].unsqueeze(2).to_broadcast([R, HB, 25])
                        last = nc.vector.tensor_tensor(oh[:, par], code, iota, ALU.is_equal)
                    last.then_inc(hot, 1)
            dve.wait_ge(counted, 8)
            nc.vector.tensor_reduce(hist[:], psh[0:25, :, 0:25].rearrange("p n b -> p b n"), AX_X, ALU.add).then_inc(summed, 1)
            dve.wait_ge(prefix, 1)
            nc.vector.tensor_reduce(base[:], psh[0:25, 0, 0:25], AX_X, ALU.add)
            nc.vector.tensor_copy(histT[:], psh[0:25, 1, 0:25]).then_inc(summed, 1)
            dve.wait_ge(prefix, 2)
            nc.vector.drain()
            nc.vector.tensor_scalar(lo[:], psh[0:25, 2, 0:25], base[:, 0:1], None, ALU.add).then_inc(summed, 1)

        @block.tensor
        def _(pe):
            pe.sem_inc(spent, 2)
            with pe.Fori(0, 4) as i:
                for par in range(2):
                    pe.wait_ge(hot, i * 2 + par + 1)
                    for c in range(HB):
                        last = nc.tensor.matmul(cols(psh[0:25, ds(i * 2 + par, 1), 0:25]), ohu[:, par, c, :], ohv[:, par, c, :],
                                                start=(c == 0), stop=(c == HB - 1))
                    last.then_inc(counted, 1)
                    nc.tensor.drain().then_inc(spent, 1)
            pe.wait_ge(summed, 1)
            nc.tensor.matmul(psh[0:25, 0, 0:25], m.below[0:25, 0:25], hist[:], start=True, stop=True)
            nc.tensor.transpose(psh[0:25, 1, 0:25], hist[:], m.ident[0:25, 0:25]).then_inc(prefix, 1)
            pe.wait_ge(summed, 2)
            nc.tensor.matmul(psh[0:25, 2, 0:25], histT[:], m.below[0:25, 0:25], start=True, stop=True).then_inc(prefix, 1)


def stage_keys(nc, m, K):
    G = NW // R
    with Stage(nc, "keys") as s:
        win = s.sb("win", [R, G, CAP, 2])
        lo, lof, at = s.sb("lo", [R, G], I32), s.sb("lof", [R, G]), s.sb("at", [R, G, CAP // ALIGN], I32)
        row0, lo_in, at_ready = s.sb("row0", [R, G]), s.sem("lo_in"), s.sem("at_ready")
        rel, b = s.sb("rel", [R, G, CAP]), s.sb("b", [R, G, CAP])
        ge0, inside = s.sb("ge0", [R, G, CAP]), s.sb("inside", [R, G, CAP])
        cnt = s.sb("cnt", [R, 1])
        pst, pss = s.ps("pst", G), s.ps("pss", 1)
        loaded, ready, turned, summed, total, copied = [s.sem(x) for x in ("loaded", "ready", "turned", "summed", "total", "copied")]
        block = s.block()

        @block.sync
        def _(sp):
            sp.dma_start(lo[:], m.LO.rearrange("u v -> (u v)").rearrange("(g p o) -> p g o", p=R, o=1), allow_slow_non_contiguous=True).then_inc(lo_in, 16)

        @block.gpsimd
        def _(pool):
            pool.wait_ge(at_ready, 1)
            rows = m.QB.rearrange("(r e) k -> r (e k)", e=ALIGN)
            for g in range(G):
                for r in range(CAP // ALIGN):
                    nc.gpsimd.indirect_dma_start(out=win[:, g, r * ALIGN:(r + 1) * ALIGN, :].rearrange("p e k -> p (e k)"), out_offset=None,
                                                 in_=rows, in_offset=bass.IndirectOffsetOnAxis(ap=at[:, g, r:r + 1], axis=0)).then_inc(loaded, 16)

        @block.vector
        def _(dve):
            dve.wait_ge(lo_in, 16)
            nc.vector.tensor_copy(lof[:], lo[:])
            nc.vector.drain()
            floor_div(nc, row0[:], lof[:], ALIGN)
            for r in range(CAP // ALIGN):
                last = nc.vector.tensor_scalar(at[:, :, r], row0[:], float(r), None, ALU.add)
            last.then_inc(at_ready, 1)
            dve.wait_ge(loaded, 16 * G * (CAP // ALIGN))
            for g in range(G):
                nc.vector.tensor_scalar(rel[:, g], win[:, g, :, 0], m.pcol[0:R, 0:1], float(QW * R * g), ALU.subtract, ALU.subtract)
            nc.vector.tensor_copy(b[:], win[:, :, :, 1]).then_inc(ready, 1)
            nc.vector.drain()
            flat = "p g e -> p (g e)"
            nc.vector.tensor_scalar(ge0[:].rearrange(flat), rel[:].rearrange(flat), 0.0, None, ALU.is_ge)
            nc.vector.drain()
            nc.vector.scalar_tensor_tensor(out=inside[:].rearrange(flat), in0=rel[:].rearrange(flat), scalar=float(QW),
                                           in1=ge0[:].rearrange(flat), op0=ALU.is_lt, op1=ALU.mult)
            nc.vector.drain()
            nc.vector.tensor_reduce(cnt[:], inside[:].rearrange(flat), AX_X, ALU.add).then_inc(summed, 1)
            dve.wait_ge(total, 1)
            nc.vector.tensor_scalar(m.flag[:], pss[0:1, 0, 0:1], float(EDGES), None, ALU.not_equal)

        @block.tensor
        def _(pe):
            pe.wait_ge(ready, 1)
            for g in range(G):
                for j, x in enumerate((rel, b)):
                    for c in range(2):
                        last = nc.tensor.transpose(pst[:, g, (2 * j + c) * R:(2 * j + c + 1) * R], x[:, g, c * P:(c + 1) * P], m.ident[0:R, 0:R])
                last.then_inc(turned, 1)
            pe.wait_ge(summed, 1)
            nc.tensor.matmul(pss[0:1, 0, 0:1], cnt[:], m.ones[0:R, 0:1], start=True, stop=True).then_inc(total, 1)

        @block.scalar
        def _(act):
            for g in range(G):
                act.wait_ge(turned, g + 1)
                nc.scalar.activation(K[:, :, g * R:(g + 1) * R], pst[:, g, 0:4 * R].rearrange("p (j w) -> p j w", j=4), ACT.Copy)


JOBS = [(j, range(4 * j, min(4 * j + 4, T))) for j in range(7)]


def stage_counts(nc, m, K):
    with Stage(nc, "counts") as s:
        ohb, ohq = s.sb("ohb", [P, 3, 2, T, R], BF16), s.sb("ohq", [P, 3, 2, T, QW], BF16)
        ct, mk = s.sb("ct", [R, 3, T, R]), s.sb("mk", [R, 3, T, R], BF16)
        ps = s.ps("ps", 7)
        neg = s.sb("neg", [R, 1])
        hot, full, free = s.sem("hot"), s.sem("full"), s.sem("free")
        ct_ready, mk_ready, looped = s.sem("ct_ready"), s.sem("mk_ready"), s.sem("looped")
        ct_out, mk_out = [s.sem(f"ct_out{n}") for n in range(3)], [s.sem(f"mk_out{n}") for n in range(3)]
        block = s.block()
        iota = m.iota[:, 0:R].unsqueeze(1).unsqueeze(1).to_broadcast([P, 2, T, R])

        @block.vector
        def _(dve):
            with dve.Fori(0, T // U) as i:
                for k in range(U):
                    t, n = i * U + k, RING3[k]
                    dve.wait_ge(full, (t + 1) * 14)
                    for oh, c0 in ((ohq, 0), (ohb, 2)):
                        code = K[:, c0:c0 + 2, ds(t * T, T)].unsqueeze(3).to_broadcast([P, 2, T, R])
                        last = nc.vector.tensor_tensor(oh[:, n], code, iota, ALU.is_equal)
                    last.then_inc(hot, 1)

        @block.tensor
        def _(pe):
            pe.sem_inc(full, 28)
            with pe.Fori(0, T // U) as i:
                for k in range(U):
                    t, n = i * U + k, RING3[k]
                    pe.wait_ge(hot, t + 1)
                    for turn, (lhs, rhs) in enumerate(((ohb, ohq), (ohq, ohb))):
                        for j, windows in JOBS:
                            pe.wait_ge(free, t * 14 + turn * 7 + j + 1)
                            for x, w in enumerate(windows):
                                for c in range(2):
                                    last = nc.tensor.matmul(ps[0:R, j, x * R:(x + 1) * R], lhs[:, n, c, w, :], rhs[:, n, c, w, :],
                                                            start=(c == 0), stop=(c == 1))
                            last.then_inc(full, 1)

        @block.scalar
        def _(act):
            act.sem_inc(free, 7)
            nc.scalar.activation(neg[:], m.ones[0:R, 0:1], ACT.Copy, scale=NEG)
            nc.scalar.drain()
            with act.Fori(0, T // U) as i:
                for k in range(U):
                    t, n = i * U + k, RING3[k]
                    act.wait_ge(ct_out[n], uses(i, k) * 32 + 32)
                    for j, windows in JOBS:
                        act.wait_ge(full, t * 14 + j + 29)
                        nw = len(windows) * W5
                        out = ct[:, n, :, 4 * j * W5:4 * j * W5 + nw]
                        last = nc.scalar.activation(out, ps[0:R, j, 0:nw * T].rearrange("p (x a) -> p a x", a=T), ACT.Copy)
                        last.then_inc(free, 1)
                    nc.scalar.drain().then_inc(ct_ready, 1)
                    act.wait_ge(mk_out[n], uses(i, k) * 32 + 32)
                    for j, windows in JOBS:
                        act.wait_ge(full, t * 14 + j + 36)
                        nw = len(windows)
                        last = nc.scalar.activation(mk[:, n, 4 * j:4 * j + nw, :], ps[0:R, j, 0:nw * R].rearrange("p (w b) -> p w b", b=R),
                                                    ACT.Relu, bias=neg[:, 0:1], scale=-NEG)
                        last.then_inc(free, 1)
                    nc.scalar.drain().then_inc(mk_ready, 1)

        @block.gpsimd
        def _(pool):
            with pool.Fori(0, T // U) as i:
                for k in range(U):
                    t, n = i * U + k, RING3[k]
                    pool.wait_ge(ct_ready, t + 1)
                    diag = cols(ct[:, n, ds(t, 1), :])
                    nc.gpsimd.tensor_tensor(diag, diag, m.ident[0:R, 0:R], ALU.add).then_inc(looped, 1)

        @block.sync
        def _(sp):
            for x in ct_out + mk_out:
                sp.sem_inc(x, 32)
            with sp.Fori(0, T // U) as i:
                for k in range(U):
                    t, n = i * U + k, RING3[k]
                    wait_apart(sp, s.tick, looped, t + 1)
                    tile_dma(sp, m.CT.rearrange("(a b) d -> b a d", b=R)[:, :, ds(t * R, R)], ct[:, n], ct_out[n])
                    wait_apart(sp, s.tick, mk_ready, t + 1)
                    tile_dma(sp, m.MK.rearrange("(t w p) b -> p t w b", t=T, p=R)[:, ds(t, 1)].rearrange("p o w b -> p (o w) b"), mk[:, n], mk_out[n])
            for n, x in enumerate(ct_out + mk_out):
                sp.wait_ge(x, 32 + 32 * RING3.count(n % 3) * (T // U))


def stage_counts_general(nc, m):
    BLOCKS = (EDGES + CAP - 1) // CAP
    with Stage(nc, "general") as s:
        e = s.sb("e", [P, 2, 2])
        relq = s.sb("relq", [P, T, 2])
        ohb, ohq = s.sb("ohb", [P, 2, R], BF16), s.sb("ohq", [P, T, 2, QW], BF16)
        ct, mk, mkb = s.sb("ct", [R, T, R]), s.sb("mk", [R, T, R]), s.sb("mkb", [R, T, R], BF16)
        ps = s.ps("ps", 7)
        loaded, hot, full, added, zeroed = [s.sem(x) for x in ("loaded", "hot", "full", "added", "zeroed")]
        finished, out = s.sem("finished"), s.sem("out")
        block = s.block()
        iota = m.iota[:, 0:R]

        def either(eng, body):
            with eng.If(eng.value_load(m.flag[0:1, 0:1], min_val=0, max_val=1)):
                body(eng)

        def dve_part(dve):
            with dve.Fori(0, T) as t:
                dve.wait_ge(out, t * 64 + 64)
                nc.vector.memset(ct[:], 0.0)
                nc.vector.memset(mk[:], 0.0).then_inc(zeroed, 1)
                with dve.Fori(0, BLOCKS) as r:
                    dve.wait_ge(loaded, t * (16 * BLOCKS) + r * 16 + 16)
                    nc.vector.tensor_tensor(relq[:], e[:, :, 0].unsqueeze(1).to_broadcast([P, T, 2]),
                                            m.wstart[:, ds(t * T, T)].unsqueeze(2).to_broadcast([P, T, 2]), ALU.subtract)
                    nc.vector.drain()
                    nc.vector.tensor_tensor(ohb[:], e[:, :, 1].unsqueeze(2).to_broadcast([P, 2, R]), iota.unsqueeze(1).to_broadcast([P, 2, R]), ALU.is_equal)
                    for c in range(2):
                        last = nc.vector.tensor_tensor(ohq[:, :, c], relq[:, :, c].unsqueeze(2).to_broadcast([P, T, QW]),
                                                       iota.unsqueeze(1).to_broadcast([P, T, QW]), ALU.is_equal)
                    last.then_inc(hot, 1)
                    dve.wait_ge(full, t * (2 * BLOCKS) + r * 2 + 1)
                    for j, windows in JOBS:
                        nw = len(windows) * W5
                        view = ct[:, :, 4 * j * W5:4 * j * W5 + nw]
                        last = nc.vector.tensor_tensor(view, view, ps[0:R, j, 0:nw * T].rearrange("p (x a) -> p a x", a=T), ALU.add)
                    last.then_inc(added, 1)
                    dve.wait_ge(full, t * (2 * BLOCKS) + r * 2 + 2)
                    for j, windows in JOBS:
                        nw = len(windows)
                        view = mk[:, 4 * j:4 * j + nw, :].rearrange("p w b -> p (w b)")
                        last = nc.vector.tensor_tensor(view, view, ps[0:R, j, 0:nw * R], ALU.add)
                    last.then_inc(added, 1)
                nc.vector.drain()
                diag = cols(ct[:, ds(t, 1), :])
                nc.vector.tensor_tensor(diag, diag, m.ident[0:R, 0:R], ALU.add)
                nc.vector.tensor_scalar(mkb[:], mk[:], 0.0, NEG, ALU.is_equal, ALU.mult).then_inc(finished, 1)

        def pe_part(pe):
            with pe.Fori(0, T) as t:
                with pe.Fori(0, BLOCKS) as r:
                    for turn in range(2):
                        pe.wait_ge(hot, t * BLOCKS + r + 1)
                        pe.wait_ge(added, t * (2 * BLOCKS) + r * 2 + turn + 1)
                        for j, windows in JOBS:
                            for x, w in enumerate(windows):
                                for c in range(2):
                                    lhs, rhs = (ohb[:, c], ohq[:, w, c]) if turn == 0 else (ohq[:, w, c], ohb[:, c])
                                    last = nc.tensor.matmul(ps[0:R, j, x * R:(x + 1) * R], lhs, rhs, start=(c == 0), stop=(c == 1))
                        last.then_inc(full, 1)

        def sp_part(sp):
            sp.sem_inc(out, 64)
            sp.sem_inc(added, 1)
            with sp.Fori(0, T) as t:
                with sp.Fori(0, BLOCKS) as r:
                    wait_apart(sp, s.tick, added, t * (2 * BLOCKS) + r * 2 + 1)
                    wait_apart(sp, s.tick, zeroed, t + 1)
                    at = sp.snap(r * CAP)
                    sp.dma_start(e[:], m.QB[ds(at, CAP)].rearrange("(p c) k -> p c k", p=P)).then_inc(loaded, 16)
                wait_apart(sp, s.tick, finished, t + 1)
                tile_dma(sp, m.CT.rearrange("(a b) d -> b a d", b=R)[:, :, ds(t * R, R)], ct[:], out)
                tile_dma(sp, m.MK.rearrange("(t w p) b -> p t w b", t=T, p=R)[:, ds(t, 1)].rearrange("p o w b -> p (o w) b"), mkb[:], out)
            sp.wait_ge(out, 64 + 64 * T)

        @block.sync
        def _(sp):
            either(sp, sp_part)

        @block.vector
        def _(dve):
            either(dve, dve_part)

        @block.tensor
        def _(pe):
            either(pe, pe_part)




def stage_stats(nc, name, rows, mean, rstd):
    with Stage(nc, name) as s:
        st = s.sb("st", [R, T, 6])
        half, var = s.sb("half", [R, T]), s.sb("var", [R, T])
        eps, std = s.sb("eps", [R, 1]), s.sb("std", [R, T])
        var_ready, std_ready = s.sem("var_ready"), s.sem("std_ready")
        block = s.block()

        @block.vector
        def _(dve):
            nc.vector.memset(eps[:], EPS)
            with dve.Fori(0, T // U) as i:
                for k in range(U):
                    nc.vector.bn_stats(cols(st[:, ds(i * U + k, 1), :]), cols(rows[:, ds(i * U + k, 1), :]))
            nc.vector.drain()
            nc.vector.tensor_tensor(mean, st[:, :, 1], st[:, :, 4], ALU.add)
            nc.vector.tensor_tensor(half[:], st[:, :, 1], st[:, :, 4], ALU.subtract)
            nc.vector.tensor_tensor(var[:], st[:, :, 2], st[:, :, 5], ALU.add)
            nc.vector.drain()
            nc.vector.tensor_scalar(mean, mean, 0.5, None, ALU.mult)
            nc.vector.tensor_tensor(half[:], half[:], half[:], ALU.mult)
            nc.vector.tensor_scalar(var[:], var[:], 1.0 / D, None, ALU.mult)
            nc.vector.drain()
            nc.vector.scalar_tensor_tensor(out=var[:], in0=half[:], scalar=0.25, in1=var[:], op0=ALU.mult, op1=ALU.add).then_inc(var_ready, 1)
            dve.wait_ge(std_ready, 1)
            nc.vector.reciprocal(rstd, std[:])

        @block.scalar
        def _(act):
            act.wait_ge(var_ready, 1)
            nc.scalar.activation(std[:], var[:], ACT.Sqrt, bias=eps[:, 0:1]).then_inc(std_ready, 1)


def stage_norm(nc, m, name, rows, mean, rstd, outT, out_rows=None, affine=None):
    with Stage(nc, name) as s:
        xn = s.sb("xn", [R, U, D])
        ps = s.ps("ps", U)
        normed, turned, free = s.sem("normed"), s.sem("turned"), s.sem("free")
        kept, loaded = s.sem("kept"), s.sem("loaded")
        if affine is not None:
            gb = s.sb("gb", [P, 4])
        block = s.block()

        @block.vector
        def _(dve):
            with dve.Fori(0, T // U) as i:
                for k in range(U):
                    t = i * U + k
                    dve.wait_ge(turned, t + 1)
                    if out_rows is not None:
                        dve.wait_ge(kept, t + 1)
                    nc.vector.tensor_scalar(xn[:, k, :], cols(rows[:, ds(t, 1), :]), mean[:, ds(t, 1)], rstd[:, ds(t, 1)],
                                            ALU.subtract, ALU.mult).then_inc(normed, 1)

        @block.tensor
        def _(pe):
            pe.sem_inc(turned, U)
            with pe.Fori(0, T // U) as i:
                for k in range(U):
                    t = i * U + k
                    pe.wait_ge(normed, t + 1)
                    pe.wait_ge(free, t + 1)
                    for c in range(2):
                        last = nc.tensor.transpose(ps[:, k, c * R:(c + 1) * R], xn[:, k, c * P:(c + 1) * P], m.ident[0:R, 0:R])
                    last.then_inc(turned, 1)

        @block.scalar
        def _(act):
            act.sem_inc(free, U)
            if affine is not None:
                act.dma_start(gb[:], affine).then_inc(loaded, 16)
                act.wait_ge(loaded, 16)
            with act.Fori(0, T // U) as i:
                for k in range(U):
                    t = i * U + k
                    act.wait_ge(turned, t + 1 + U)
                    if affine is None:
                        last = nc.scalar.activation(outT[:, :, ds(t * R, R)], ps[:, k, 0:2 * R].rearrange("p (c n) -> p c n", c=2), ACT.Copy)
                    else:
                        for c in range(2):
                            last = nc.scalar.activation(outT[:, c, ds(t * R, R)], ps[:, k, c * R:(c + 1) * R], ACT.Identity,
                                                        bias=gb[:, 2 + c:3 + c], scale=gb[:, c:c + 1])
                    last.then_inc(free, 1)

        if out_rows is not None:
            @block.gpsimd
            def _(pool):
                pool.sem_inc(kept, U)
                with pool.Fori(0, T // U) as i:
                    for k in range(U):
                        t = i * U + k
                        pool.wait_ge(normed, t + 1)
                        nc.gpsimd.tensor_copy(cols(out_rows[:, ds(t, 1), :]), xn[:, k, :]).then_inc(kept, 1)


CHUNKS, STRIDE = 8, 390
WIDE = N - (CHUNKS - 1) * STRIDE


def stage_linear(nc, name, xT, KC, w, bias, MC, func, outT):
    with Stage(nc, name) as s:
        wt, bt = s.sb("w", [P, KC, MC * P]), s.sb("b", [P, MC])
        ps = s.ps("ps", 2 * MC)
        loaded, full, free = s.sem("loaded"), s.sem("full"), s.sem("free")
        block = s.block()

        @block.sync
        def _(sp):
            sp.dma_start(wt[:], w.rearrange("(c p) n -> p c n", p=P)).then_inc(loaded, 16)
            sp.dma_start(bt[:], bias).then_inc(loaded, 16)

        @block.tensor
        def _(pe):
            pe.wait_ge(loaded, 32)
            with pe.Fori(0, CHUNKS // 2) as i:
                for par in range(2):
                    for o in range(MC):
                        pe.wait_ge(free, (i * 2 + par) * MC + o + 1)
                        for c in range(KC):
                            last = nc.tensor.matmul(ps[:, par * MC + o, 0:WIDE], wt[:, c, o * P:(o + 1) * P],
                                                    xT[:, c, ds((i * 2 + par) * STRIDE, WIDE)], start=(c == 0), stop=(c == KC - 1))
                        last.then_inc(full, 1)

        @block.scalar
        def _(act):
            act.sem_inc(free, 2 * MC)
            act.wait_ge(loaded, 32)
            with act.Fori(0, CHUNKS // 2) as i:
                for par in range(2):
                    for o in range(MC):
                        nc.scalar.drain()
                        act.wait_ge(full, (i * 2 + par) * MC + o + 1)
                        nc.scalar.activation(outT[:, o, ds((i * 2 + par) * STRIDE, WIDE)], ps[:, par * MC + o, 0:WIDE], func,
                                             bias=bt[:, o:o + 1]).then_inc(free, 1)


class RowProducts:

    def __init__(self, nc, s, sources, outs, readers, setup=None):
        self.nc, self.outs, self.setup = nc, outs, setup
        self.sources = sources
        self.chunks = sum(c for _, c in sources)
        self.xs = s.sb("xs", [P, U, self.chunks, R])
        self.ps = s.ps("ps", 3 * len(outs))
        self.staged, self.full = s.sem("staged"), s.sem("full")
        self.free = [s.sem(f"free{n}") for n in range(readers)]

    def bank(self, k, o):
        return RING3[k] * len(self.outs) + o

    def psum(self, k, o):
        return self.ps[0:R, self.bank(k, o), 0:self.outs[o][0]]

    def stage(self, pool):
        nc = self.nc
        with pool.Fori(0, T // U) as i:
            for k in range(U):
                t = i * U + k
                pool.wait_ge(self.full, t + 1)
                c0 = 0
                for xT, chunks in self.sources:
                    K = xT.shape[0]
                    last = nc.gpsimd.tensor_copy(self.xs[0:K, k, c0:c0 + chunks, :], xT[:, :, ds(t * R, R)])
                    c0 += chunks
                last.then_inc(self.staged, 1)

    def multiply(self, pe):
        nc = self.nc
        pe.sem_inc(self.full, U)
        if self.setup is not None:
            self.setup(pe)
        with pe.Fori(0, T // U) as i:
            for k in range(U):
                t = i * U + k
                pe.wait_ge(self.staged, t + 1)
                for free in self.free:
                    pe.wait_ge(free, t + 1)
                for o, (width, rhs) in enumerate(self.outs):
                    for c, right in enumerate(rhs):
                        last = nc.tensor.matmul(self.psum(k, o), self.xs[0:right.shape[0], k, c, :], right,
                                                start=(c == 0), stop=(c == len(rhs) - 1))
                last.then_inc(self.full, 1)

    def read(self, eng, body, reader=0):
        eng.sem_inc(self.free[reader], 2)
        with eng.Fori(0, T // U) as i:
            for k in range(U):
                eng.wait_ge(self.full, i * U + k + 1 + U)
                body(i, k, i * U + k).then_inc(self.free[reader], 1)



QUARTERS, QSTRIDE = 4, 781
QW4 = N - (QUARTERS - 1) * QSTRIDE
HB = QW4 // 2


def stage_gat_project(nc, m, g, xT, KC, w, att_s, att_d, AL):
    H, F, HF = g.heads, g.feat, g.heads * g.feat
    with Stage(nc, g.name + "p") as s:
        wt = s.sb("w", [P, KC, HF])
        att, prod = s.sb("att", [P, 2, HF]), s.sb("prod", [P, 2, HF])
        wa = s.sb("wa", [P, KC, 2 * H])
        hx = s.sb("hx", [R, U, g.row])
        loaded, folded, ones_set = s.sem("loaded"), s.sem("folded"), s.sem("ones_set")
        h_ready, al_ready = s.sem("h_ready"), s.sem("al_ready")
        out = [s.sem(f"out{k}") for k in range(U)]

        def setup(pe):
            pe.wait_ge(loaded, 48)
            pe.wait_ge(folded, 1)
        rp = RowProducts(nc, s, [(xT, KC)], [(HF, [wt[:, c, :] for c in range(KC)]), (2 * H, [wa[:, c, :] for c in range(KC)])], 2, setup)
        block = s.block()

        @block.sync
        def _(sp):
            for x in out:
                sp.sem_inc(x, 32)
            sp.dma_start(wt[:], w.rearrange("(c p) n -> p c n", p=P)).then_inc(loaded, 16)
            for j, a in enumerate((att_s, att_d)):
                sp.dma_start(att[:, j, :], a.rearrange("h f -> (h f)").partition_broadcast(P)).then_inc(loaded, 16)
            with sp.Fori(0, T // U) as i:
                for k in range(U):
                    t = i * U + k
                    wait_apart(sp, s.tick, h_ready, t + 1)
                    wait_apart(sp, s.tick, al_ready, t + 1)
                    tile_dma(sp, g.HX.rearrange("(t p) n -> p t n", p=R)[:, ds(t, 1)].rearrange("p o n -> p (o n)"), hx[:, k], out[k])
            for x in out:
                sp.wait_ge(x, 32 + 32 * (T // U))

        @block.gpsimd
        def _(pool):
            if g.ones_in_rows:
                nc.gpsimd.memset(hx[:], 1.0).then_inc(ones_set, 1)
            rp.stage(pool)

        @block.tensor
        def _(pe):
            rp.multiply(pe)

        @block.vector
        def _(dve):
            dve.wait_ge(loaded, 48)
            for c in range(KC):
                for j in range(2):
                    nc.vector.tensor_tensor(prod[:, j, :], wt[:, c, :], att[:, j, :], ALU.mult)
                nc.vector.drain()
                last = nc.vector.tensor_reduce(wa[:, c, :], prod[:].rearrange("p j (h f) -> p (j h) f", h=H), AX_X, ALU.add)
                if c < KC - 1:
                    nc.vector.drain()
            last.then_inc(folded, 1)

            if g.ones_in_rows:
                dve.wait_ge(ones_set, 1)

            def scores(i, k, t):
                dve.wait_ge(out[k], (i + 1) * 32)
                ps = rp.psum(k, 1)
                nc.vector.tensor_copy(AL[:, :, ds(t, 1)], ps.unsqueeze(2))
                nc.vector.tensor_copy(hx[:, k, g.row - 2 * H:g.row - H], ps[:, 0:H])
                last = nc.vector.tensor_scalar(hx[:, k, g.row - H:g.row], ps[:, 0:H], 0.2, None, ALU.mult)
                nc.vector.drain().then_inc(al_ready, 1)
                return nc.vector.drain()
            rp.read(dve, scores, 1)

        @block.scalar
        def _(act):
            if g.ones_in_rows:
                act.wait_ge(ones_set, 1)

            def project(i, k, t):
                act.wait_ge(out[k], (i + 1) * 32)
                dst = hx[:, k, 0:g.row - 2 * H]
                if g.ones_in_rows:
                    dst = dst.rearrange("p (h f) -> p h f", h=H)[:, :, 0:F]
                    nc.scalar.activation(dst, rp.psum(k, 0).rearrange("p (h f) -> p h f", h=H), ACT.Copy)
                else:
                    nc.scalar.activation(dst, rp.psum(k, 0), ACT.Copy)
                nc.scalar.drain().then_inc(h_ready, 1)
                return nc.scalar.drain()
            rp.read(act, project, 0)


def stage_rows_out(nc, m, name, pieces):
    with Stage(nc, name) as s:
        n = len(pieces)
        ht = pieces[0][0].shape[1] * T
        buf = s.sb("buf", [ht, n, R])
        ps = s.ps("ps", n)
        turned, copied, out = s.sem("turned"), s.sem("copied"), s.sem("out")
        block = s.block()

        @block.tensor
        def _(pe):
            for j, (x, _) in enumerate(pieces):
                nc.tensor.transpose(ps[0:ht, j, 0:R], x.rearrange("p h t -> p (h t)"), m.ident[0:R, 0:R]).then_inc(turned, 1)

        @block.scalar
        def _(act):
            for j in range(n):
                act.wait_ge(turned, j + 1)
                nc.scalar.activation(buf[:, j, :], ps[0:ht, j, 0:R], ACT.Copy).then_inc(copied, 1)

        @block.sync
        def _(sp):
            for j, (_, dram) in enumerate(pieces):
                sp.wait_ge(copied, j + 1)
                sp.dma_start(dram, buf[:, j, :]).then_inc(out, 16)
            sp.wait_ge(out, 16 * n)


def level_of_max(nc, AL, UV, h0, h1, H, z, z2):
    ald = AL[:, H + h0:H + h1, :]
    nc.vector.tensor_tensor(z[:], z[:], ald, ALU.add)
    nc.vector.drain()
    nc.vector.tensor_scalar(z2[:], z[:], 0.2, None, ALU.mult)
    nc.vector.drain()
    nc.vector.tensor_tensor(z[:], z[:], z2[:], ALU.max)
    nc.vector.drain()
    nc.vector.tensor_tensor(UV[:, 0, h0:h1], ald, z[:], ALU.subtract)
    nc.vector.scalar_tensor_tensor(out=UV[:, 1, h0:h1], in0=ald, scalar=0.2, in1=z[:], op0=ALU.mult, op1=ALU.subtract)


def stage_gat_max(nc, m, g, AL, UV, heads):
    H = heads
    with Stage(nc, g.name + "m") as s:
        als, mk = s.sb("als", [R, H, N]), s.sb("mk", [R, 3, N], BF16)
        junk, top = s.sb("junk", [R, H, N], BF16), s.sb("top", [R, U, H])
        z, z2 = s.sb("z", [R, H, T]), s.sb("z2", [R, H, T])
        als_in, used = s.sem("als_in"), s.sem("used")
        mk_in = [s.sem(f"mk_in{n}") for n in range(3)]
        block = s.block()

        @block.sync
        def _(sp):
            for h in range(H):
                row = m.ALS[h * T:(h + 1) * T].rearrange("t r -> (t r)").partition_broadcast(R)
                tile_dma(sp, als[:, h, :], row, als_in)
            with sp.Fori(0, T // U) as i:
                for k in range(U):
                    t, n = i * U + k, RING3[k]
                    wait_apart(sp, s.tick, used, t + 1)
                    tile_dma(sp, mk[:, n, :], m.MK.rearrange("(t p c) b -> p t (c b)", t=T, c=T)[:, ds(t, 1)].rearrange("p o n -> p (o n)"), mk_in[n])

        @block.vector
        def _(dve):
            dve.sem_inc(used, 2)
            dve.wait_ge(als_in, 32 * H)
            with dve.Fori(0, T // U) as i:
                for k in range(U):
                    t, n = i * U + k, RING3[k]
                    wait_apart(dve, s.tick, mk_in[n], uses(i, k) * 32 + 32)
                    for h in range(H):
                        nc.vector.tensor_tensor_reduce(out=junk[:, h, :], in0=als[:, h, :], in1=mk[:, n, :], scale=1.0, scalar=-3e38,
                                                       op0=ALU.subtract, op1=ALU.max, accum_out=top[:, k, h:h + 1])
                    nc.vector.drain()
                    nc.vector.tensor_tensor(z[:, :, ds(t, 1)], top[:, k, :].unsqueeze(2), AL[:, 0:H, ds(t, 1)], ALU.max)
                    nc.vector.drain().then_inc(used, 1)
            level_of_max(nc, AL, UV, 0, H, g.heads, z, z2)


def stage_gat_attend(nc, m, g, bias, OT, g0, g1, AL=None, UV=None):
    H, F, HG = g.heads, g.feat, g.group
    ahead = AL is not None
    blocks = [1 if g.ones_in_rows else F // P + 1] * HG
    with Stage(nc, f"{g.name}a{g0}") as s:
        x = s.sb("x", [R, 3, HG, QW4])
        ct = s.sb("ct", [R, U, QW4])
        hx = s.sb("hx", [R, U, g.row])
        uv = s.sb("uv", [R, 2, 2, HG, QW4])
        PF = F if g.ones_in_rows else P
        den, y = s.sb("den", [PF, HG, QW4]), s.sb("y", [PF, HG if g.out == "elu" else 1, QW4])
        bt = s.sb("bt", list(bias.shape))
        ps = s.ps("ps", 2 * sum(blocks))
        if ahead:
            h0, h1 = g1 * HG, (g1 + 1) * HG
            als, mk = s.sb("als", [R, 2, HG, QW4]), s.sb("mk", [R, 3, QW4], BF16)
            junk, top = s.sb("junk", [R, HG, QW4], BF16), s.sb("top", [R, U, HG])
            z, z2 = s.sb("z", [R, HG, T]), s.sb("z2", [R, HG, T])
            als_in, mk_in = [s.sem(f"als_in{p}") for p in range(2)], [s.sem(f"mk_in{n}") for n in range(3)]
            mk_used = s.sem("mk_used")
            MKv = m.MK.rearrange("(t p c) b -> p t (c b)", t=T, c=T)
            ALSv = m.ALS[0:H * T].rearrange("(h t) r -> h (t r)", t=T)
        bias_in = s.sem("bias_in")
        uv_in = [s.sem(f"uv_in{p}") for p in range(2)]
        ct_in, hx_in = [s.sem(f"ct_in{k}") for k in range(U)], [s.sem(f"hx_in{k}") for k in range(U)]
        linear_ready, score_ready, exp_ready, weight_ready = [s.sem(n) for n in ("linear_ready", "score_ready", "exp_ready", "weight_ready")]
        spent, quarter_done, summed = [s.sem(n) for n in ("spent", "quarter_done", "summed")]
        nums_out, dens_out, finished = s.sem("nums_out"), s.sem("dens_out"), s.sem("finished")
        low_ready, low_exp = s.sem("low_ready"), s.sem("low_exp")
        block = s.block()
        CTv = m.CT.rearrange("(a b) d -> b a d", b=R)
        HXv = g.HX.rearrange("(a b) n -> b a n", b=R)
        UVv = m.UV.rearrange("j (h t) r -> j h (t r)", t=T)

        def passes(eng, tile, before=None, after=None):
            for gi in range(g0, g1):
                with eng.Fori(0, QUARTERS // 2) as qq:
                    for par in range(2):
                        q = (gi - g0) * QUARTERS + qq * 2 + par
                        if before is not None:
                            before(gi, q, qq, par)
                        for k in range(U):
                            tile(gi, q, par, 0, k, k == 0, False)
                        with eng.Fori(1, T // U - 1) as j:
                            for k in range(U):
                                tile(gi, q, par, j, k, False, False)
                        for k in range(U):
                            tile(gi, q, par, T // U - 1, k, False, k == U - 1)
                        if after is not None:
                            after(gi, q, qq, par)

        @block.sync
        def _(sp):
            sp.dma_start(bt[:], bias).then_inc(bias_in, 16)

            def quarter(gi, q, qq, par):
                wait_apart(sp, s.tick, quarter_done, q + 1)
                for j in range(2):
                    src = UVv[j, gi * HG:(gi + 1) * HG, ds((qq * 2 + par) * QSTRIDE, QW4)].unsqueeze(0)
                    src = src.to_broadcast([R, HG, QW4])
                    tile_dma(sp, uv[:, par, j], src, uv_in[par])
                if ahead:
                    src = ALSv[h0:h1, ds((qq * 2 + par) * QSTRIDE, QW4)].unsqueeze(0).to_broadcast([R, HG, QW4])
                    tile_dma(sp, als[:, par], src, als_in[par])

            def tile(gi, q, par, j, k, first, last):
                wait_apart(sp, s.tick, spent, q * T + j * U + k + 1)
                a = j * U + k
                d0 = (q - (gi - g0) * QUARTERS) * QSTRIDE
                tile_dma(sp, ct[:, k, :], CTv[:, ds(a, 1), ds(d0, QW4)].rearrange("p o n -> p (o n)"), ct_in[k])
                tile_dma(sp, hx[:, k, :], HXv[:, ds(a, 1), :].rearrange("p o n -> p (o n)"), hx_in[k])
                if ahead:
                    wait_apart(sp, s.tick, mk_used, q * T + j * U + k + 1)
                    tile_dma(sp, mk[:, RING3[k], :], MKv[:, ds(a, 1), ds(d0, QW4)].rearrange("p o n -> p (o n)"), mk_in[RING3[k]])
            passes(sp, tile, quarter)

        @block.scalar
        def _(act):
            def quarter(gi, q, qq, par):
                act.wait_ge(uv_in[par], ((gi - g0) * (QUARTERS // 2) + qq + 1) * 64)

            def exp_low(q):
                for h in range(HG):
                    act.wait_ge(low_ready, q * HG + h + 1)
                    nc.scalar.activation(den[:, h, :], den[:, h, :], ACT.Exp).then_inc(low_exp, 1)

            def tile(gi, q, par, j, k, first, last):
                n = q * T + j * U + k
                act.wait_ge(hx_in[k], (q * (T // U) + j + 1) * 32)
                act.wait_ge(spent, n + U - 1)
                for h in range(HG):
                    col = g.row - H + gi * HG + h
                    nc.scalar.activation(x[:, RING3[k], h, :], uv[:, par, 1, h, :], ACT.Identity, bias=hx[:, k, col:col + 1]).then_inc(linear_ready, 1)
                for h in range(HG):
                    act.wait_ge(score_ready, n * HG + h + 1)
                    nc.scalar.activation(x[:, RING3[k], h, :], x[:, RING3[k], h, :], ACT.Exp).then_inc(exp_ready, 1)
                if g.out == "elu" and isinstance(j, int) and j == 0 and k == U - 1:
                    exp_low(q)

            def finish(gi, q, qq, par):
                act.wait_ge(finished, q + 1)
                act.wait_ge(summed, q + 1)
                for h in range(HG):
                    b0 = 2 * sum(blocks[:h])
                    for f in range(1 if g.ones_in_rows else blocks[h] - 1):
                        num = ps[0:PF, b0 + 2 * f:b0 + 2 * f + 2, 0:HB]
                        dst = OT[:, gi * HG + h + f, ds((qq * 2 + par) * QSTRIDE, QW4)]
                        nc.scalar.activation(dst.rearrange("p (b n) -> p b n", b=2), num, ACT.Copy)
                nc.scalar.drain().then_inc(nums_out, 1)

            act.sem_inc(nums_out, 1)
            if g.out == "elu":
                act.wait_ge(low_ready, HG)
            passes(act, tile, quarter, finish)
            if g.out == "elu":
                exp_low((g1 - g0) * QUARTERS)

        @block.vector
        def _(dve):
            dve.sem_inc(quarter_done, 2)
            if ahead:
                dve.sem_inc(mk_used, 2)
                nc.vector.tensor_copy(z[:], AL[:, h0:h1, :])
                nc.vector.drain()

            def quarter(gi, q, qq, par):
                if ahead:
                    wait_apart(dve, s.tick, als_in[par], (qq + 1) * 32)
            dve.sem_inc(dens_out, 1)

            def tile(gi, q, par, j, k, first, last):
                n = q * T + j * U + k

                def maximum(h):
                    nc.vector.tensor_tensor_reduce(out=junk[:, h, :], in0=als[:, par, h, :], in1=mk[:, RING3[k], :], scale=1.0, scalar=-3e38,
                                                   op0=ALU.subtract, op1=ALU.max, accum_out=top[:, k, h:h + 1])

                for h in range(HG):
                    dve.wait_ge(linear_ready, n * HG + h + 1)
                    col = g.row - 2 * H + gi * HG + h
                    xh = x[:, RING3[k], h, :]
                    nc.vector.scalar_tensor_tensor(out=xh, in0=uv[:, par, 0, h, :], scalar=hx[:, k, col:col + 1], in1=xh,
                                                   op0=ALU.add, op1=ALU.max).then_inc(score_ready, 1)
                if ahead:
                    wait_apart(dve, s.tick, mk_in[RING3[k]], uses(q * (T // U) + j, k) * 32 + 32)
                    maximum(0)
                dve.wait_ge(ct_in[k], (q * (T // U) + j + 1) * 32)
                for h in range(HG):
                    dve.wait_ge(exp_ready, n * HG + h + 1)
                    xh = x[:, RING3[k], h, :]
                    nc.vector.scalar_tensor_tensor(out=xh, in0=xh, scalar=1.0, in1=ct[:, k, :], op0=ALU.min, op1=ALU.mult).then_inc(weight_ready, 1)
                if ahead:
                    for h in range(1, HG):
                        maximum(h)
                    nc.vector.drain().then_inc(mk_used, 1)
                    if k == U - 1:
                        zt = z[:, :, ds(j * U, U)]
                        nc.vector.tensor_tensor(zt, top[:].rearrange("p k h -> p h k"), zt, ALU.max)
                        nc.vector.drain()

            def finish(gi, q, qq, par):
                nc.vector.drain().then_inc(quarter_done, 1)
                dve.wait_ge(finished, q + 1)
                dve.wait_ge(summed, q + 1)
                for h in range(HG):
                    b0 = 2 * sum(blocks[:h])
                    src = ps[PF:2 * PF, b0:b0 + 2, 0:HB] if g.ones_in_rows else ps[:, b0 + 2 * blocks[h] - 2:b0 + 2 * blocks[h], 0:HB]
                    nc.vector.reciprocal(den[:, h, :].rearrange("p (b n) -> p b n", b=2), src)
                nc.vector.drain().then_inc(dens_out, 1)
            passes(dve, tile, quarter, finish)
            if ahead:
                level_of_max(nc, AL, UV, h0, h1, H, z, z2)

        @block.gpsimd
        def _(pool):
            pool.wait_ge(bias_in, 16)
            if g.out == "elu":
                nc.gpsimd.memset(den[:], 0.0).then_inc(low_ready, HG)
            pool.sem_inc(finished, 1)
            for gi in range(g0, g1):
                with pool.Fori(0, QUARTERS // 2) as qq:
                    for par in range(2):
                        q = (gi - g0) * QUARTERS + qq * 2 + par
                        pool.wait_ge(nums_out, q + 2)
                        pool.wait_ge(dens_out, q + 2)
                        columns = ds((qq * 2 + par) * QSTRIDE, QW4)
                        for h in range(HG):
                            for f in range(1 if g.ones_in_rows else blocks[h] - 1):
                                head = gi * HG + h + f
                                bcol, dst = bt[:, head:head + 1], OT[:, head, columns]
                                yh = y[:, h if g.out == "elu" else 0, :]
                                nc.gpsimd.tensor_tensor(yh, dst, den[:, h, :], ALU.mult)
                                nc.gpsimd.drain()
                                if g.out == "relu":
                                    nc.gpsimd.tensor_scalar(yh, yh, bcol, 0.0, ALU.add, ALU.max)
                                else:
                                    nc.gpsimd.tensor_scalar(yh, yh, bcol, None, ALU.add)
                                nc.gpsimd.drain()
                                if g.out == "elu":
                                    nc.gpsimd.tensor_scalar(den[:, h, :], yh, 0.0, None, ALU.min).then_inc(low_ready, 1)
                                else:
                                    nc.gpsimd.tensor_copy(dst, yh)
                                    nc.gpsimd.drain()
                        if g.out == "elu":
                            for h in range(HG):
                                nc.gpsimd.tensor_scalar(y[:, h, :], y[:, h, :], 0.0, 1.0, ALU.max, ALU.subtract)
                                nc.gpsimd.drain()
                                wait_apart(pool, s.tick, low_exp, (q + 1) * HG + h + 1)
                                nc.gpsimd.tensor_tensor(OT[:, gi * HG + h, columns], y[:, h, :], den[:, h, :], ALU.add)
                        nc.gpsimd.drain().then_inc(finished, 1)

        @block.tensor
        def _(pe):
            pe.sem_inc(spent, U)

            def quarter(gi, q, qq, par):
                pe.wait_ge(nums_out, q + 1)
                pe.wait_ge(dens_out, q + 1)

            def tile(gi, q, par, j, k, first, last):
                n = q * T + j * U + k
                for h in range(HG):
                    pe.wait_ge(weight_ready, n * HG + h + 1)
                    b0 = 2 * sum(blocks[:h])
                    head = gi * HG + h
                    if g.ones_in_rows:
                        left = [hx[:, k, head * P:(head + 1) * P]]
                    else:
                        left = [hx[:, k, head * F + f * P:head * F + (f + 1) * P] for f in range(F // P)] + [m.ones[0:R, :]]
                    for f, lhs in enumerate(left):
                        for half in range(2):
                            mm = nc.tensor.matmul(ps[:, b0 + 2 * f + half, 0:HB], lhs, x[:, RING3[k], h, half * HB:(half + 1) * HB],
                                                  start=first, stop=last)
                mm.then_inc(spent, 1)

            def finish(gi, q, qq, par):
                nc.tensor.drain().then_inc(summed, 1)
            passes(pe, tile, quarter, finish)


class Gat:

    def __init__(self, nc, name, heads, feat, group, out):
        self.name, self.heads, self.feat, self.group, self.out = name, heads, feat, group, out
        self.max_ahead = heads == 2 * group and feat >= P
        self.ones_in_rows = feat < P
        self.row = (heads * P if self.ones_in_rows else heads * feat) + 2 * heads
        self.HX = nc.dram_tensor(f"{name}_rows", [N, self.row], F32).ap()


def graph_attention(nc, m, g, AL, bias, OT):
    ht, G, first = g.heads * T, g.heads // g.group, g.group * T
    with ExitStack() as c:
        UV = c.enter_context(nc.sbuf_tensor(f"{g.name}_UV", [R, 2, g.heads, T], F32))[:]
        stage_rows_out(nc, m, g.name + "s", [(AL[:, 0:g.heads, :], m.ALS[0:ht])])
        if g.max_ahead:
            stage_gat_max(nc, m, g, AL, UV, g.group)
            stage_rows_out(nc, m, g.name + "u", [(UV[:, 0, 0:g.group], m.UV[0, 0:first]), (UV[:, 1, 0:g.group], m.UV[1, 0:first])])
            stage_gat_attend(nc, m, g, bias, OT, 0, 1, AL, UV)
            stage_rows_out(nc, m, g.name + "v", [(UV[:, j, g.group:], m.UV[j, first:ht]) for j in range(2)])
        else:
            stage_gat_max(nc, m, g, AL, UV, g.heads)
            stage_rows_out(nc, m, g.name + "u", [(UV[:, 0], m.UV[0, 0:ht]), (UV[:, 1], m.UV[1, 0:ht])])
    stage_gat_attend(nc, m, g, bias, OT, 1 if g.max_ahead else 0, G)


def stage_add_transposed(nc, m, name, srcT, K, chunks, X):
    with Stage(nc, name) as s:
        xs = s.sb("xs", [K, U, chunks, R])
        ps = s.ps("ps", U)
        staged, turned, free = s.sem("staged"), s.sem("turned"), s.sem("free")
        block = s.block()

        @block.gpsimd
        def _(pool):
            with pool.Fori(0, T // U) as i:
                for k in range(U):
                    t = i * U + k
                    pool.wait_ge(turned, t + 1)
                    nc.gpsimd.tensor_copy(xs[:, k], srcT[:, :, ds(t * R, R)]).then_inc(staged, 1)

        @block.tensor
        def _(pe):
            pe.sem_inc(turned, U)
            with pe.Fori(0, T // U) as i:
                for k in range(U):
                    t = i * U + k
                    pe.wait_ge(staged, t + 1)
                    wait_apart(pe, s.tick, free, t + 1)
                    for c in range(chunks):
                        last = nc.tensor.transpose(ps[0:R, k, c * K:(c + 1) * K], xs[:, k, c, :], m.ident[0:K, 0:K])
                    last.then_inc(turned, 1)

        @block.vector
        def _(dve):
            dve.sem_inc(free, U)
            with dve.Fori(0, T // U) as i:
                for k in range(U):
                    t = i * U + k
                    dve.wait_ge(turned, t + 1 + U)
                    xt = cols(X[:, ds(t, 1), :])
                    nc.vector.tensor_tensor(xt, xt, ps[0:R, k, 0:D], ALU.add).then_inc(free, 1)


def stage_add_row(nc, name, vectors, X, more=None):
    with Stage(nc, name) as s:
        vt = s.sb("v", [R, len(vectors), D])
        loaded = s.sem("loaded")
        block = s.block()

        @block.sync
        def _(sp):
            for j, v in enumerate(vectors):
                sp.dma_start(vt[:, j, :], v.partition_broadcast(R)).then_inc(loaded, 16)

        @block.vector
        def _(dve):
            dve.wait_ge(loaded, 16 * len(vectors))
            if more is not None:
                nc.vector.tensor_tensor(X, X, more, ALU.add)
                nc.vector.drain()
            for j in range(len(vectors)):
                nc.vector.tensor_tensor(X, X, vt[:, j, :].unsqueeze(1).to_broadcast([R, T, D]), ALU.add)
                nc.vector.drain()




def stage_mix(nc, m, a, xmT, XN):
    KR, HEADS, DH = 4, 8, 32
    J = HEADS * KR
    with ExitStack() as c:
        sb = lambda n, shape: c.enter_context(nc.sbuf_tensor(f"mix_{n}", shape, F32))
        QK, V = sb("QK", [R, T, 2 * J]), sb("V", [R, T, D + 1])
        KVO = sb("KVO", [J + 1, D])

        with Stage(nc, "mixp") as s:
            w = s.sb("w", [P, 2, 2 * J + D])
            zeroed, loaded = s.sem("zeroed"), s.sem("loaded")

            def setup(pe):
                pe.wait_ge(loaded, 16 * 3 * HEADS)
            rp = RowProducts(nc, s, [(xmT, 2)], [(2 * J, [w[:, x, 0:2 * J] for x in range(2)]), (D, [w[:, x, 2 * J:] for x in range(2)])], 2, setup)
            block = s.block()

            @block.sync
            def _(sp):
                sp.wait_ge(zeroed, 1)
                for h in range(HEADS):
                    p0, x = h * DH % P, h * DH // P
                    for wh, c0, n in ((a["L0_mix_Wq"], h * KR, KR), (a["L0_mix_Wk"], J + h * KR, KR), (a["L0_mix_Wv"], 2 * J + h * DH, DH)):
                        sp.dma_start(w[p0:p0 + DH, x, c0:c0 + n], wh).then_inc(loaded, 16)

            @block.gpsimd
            def _(pool):
                nc.gpsimd.memset(w[:], 0.0).then_inc(zeroed, 1)
                nc.gpsimd.memset(V[:, :, D:D + 1], 1.0)
                rp.stage(pool)

            @block.tensor
            def _(pe):
                rp.multiply(pe)

            @block.vector
            def _(dve):
                rp.read(dve, lambda i, k, t: nc.vector.tensor_copy(cols(QK[:, ds(t, 1), :]), rp.psum(k, 0)))

            @block.scalar
            def _(act):
                rp.read(act, lambda i, k, t: nc.scalar.activation(cols(V[:, ds(t, 1), 0:D]), rp.psum(k, 1), ACT.Copy), 1)

        with Stage(nc, "mixs") as s:
            q, k = QK[:, :, 0:J], QK[:, :, J:2 * J]
            red = s.sb("red", [R, T, HEADS])
            kmax, kmaxT, diag = s.sb("kmax", [R, J]), s.sb("kmaxT", [J, 1]), s.sb("diag", [J, J])
            kv, kvT, inv, wo = s.sb("kv", [J, D]), s.sb("kvT", [P, 2, J]), s.sb("inv", [J, 1]), s.sb("wo", [P, 2, D])
            ps = s.ps("ps", 6)
            step, mul, ex, loaded = s.sem("step"), s.sem("mul"), s.sem("ex"), s.sem("loaded")
            block = s.block()
            q4 = q.rearrange("p t (h r) -> p t h r", r=KR)

            @block.sync
            def _(sp):
                sp.dma_start(wo[:], a["L0_mix_Wo"].rearrange("(c p) n -> p c n", p=P)).then_inc(loaded, 16)
                sp.dma_start(KVO[J:J + 1, :], a["L0_mix_bo"].unsqueeze(0)).then_inc(loaded, 16)
                sp.wait_ge(loaded, 32)

            @block.vector
            def _(dve):
                nc.vector.tensor_reduce(kmax[:], k.rearrange("p t j -> p j t"), AX_X, ALU.max).then_inc(step, 1)
                nc.vector.tensor_reduce(red[:], q4, AX_X, ALU.max)
                nc.vector.drain()
                nc.vector.tensor_tensor(q4, q4, red[:].unsqueeze(3).to_broadcast([R, T, HEADS, KR]), ALU.subtract).then_inc(step, 1)
                dve.wait_ge(mul, 1)
                nc.vector.tensor_reduce(kmaxT[:], ps[0:J, 0, 0:R], AX_X, ALU.max)
                nc.vector.drain()
                nc.vector.tensor_scalar(diag[:], m.ident[0:J, 0:J], kmaxT[:, 0:1], None, ALU.mult).then_inc(step, 1)
                dve.wait_ge(mul, 2)
                nc.vector.tensor_tensor(k, k, ps[0:R, 1, 0:J].unsqueeze(1).to_broadcast([R, T, J]), ALU.subtract).then_inc(step, 1)
                dve.wait_ge(ex, 1)
                nc.vector.tensor_reduce(red[:], q4, AX_X, ALU.add)
                nc.vector.drain()
                nc.vector.reciprocal(red[:], red[:])
                nc.vector.drain()
                nc.vector.tensor_tensor(q4, q4, red[:].unsqueeze(3).to_broadcast([R, T, HEADS, KR]), ALU.mult)
                dve.wait_ge(mul, 3)
                nc.vector.reciprocal(inv[:], ps[0:J, 2, D:D + 1])
                nc.vector.drain()
                nc.vector.scalar_tensor_tensor(out=kv[:], in0=ps[0:J, 2, 0:D], scalar=inv[:, 0:1], in1=m.headmask[0:J, :],
                                               op0=ALU.mult, op1=ALU.mult).then_inc(step, 1)
                dve.wait_ge(mul, 4)
                nc.vector.tensor_copy(kvT[:], ps[:, 3, 0:2 * J].rearrange("p (c j) -> p c j", c=2)).then_inc(step, 1)
                dve.wait_ge(mul, 5)
                nc.vector.tensor_copy(KVO[0:J, :], ps[0:J, 4, 0:D])

            @block.scalar
            def _(act):
                act.wait_ge(step, 2)
                nc.scalar.activation(q, q, ACT.Exp).then_inc(ex, 1)
                act.wait_ge(step, 4)
                nc.scalar.activation(k, k, ACT.Exp).then_inc(ex, 1)

            @block.tensor
            def _(pe):
                pe.wait_ge(step, 1)
                nc.tensor.transpose(ps[0:J, 0, 0:R], kmax[:], m.ident[0:R, 0:R]).then_inc(mul, 1)
                pe.wait_ge(step, 3)
                nc.tensor.matmul(ps[0:R, 1, 0:J], m.ones[0:J, 0:R], diag[:], start=True, stop=True).then_inc(mul, 1)
                pe.wait_ge(ex, 2)
                for t in range(T):
                    last = nc.tensor.matmul(ps[0:J, 2, 0:D + 1], k[:, t, :], V[:, t, :], start=(t == 0), stop=(t == T - 1))
                last.then_inc(mul, 1)
                pe.wait_ge(step, 5)
                for x in range(2):
                    last = nc.tensor.transpose(ps[:, 3, x * J:(x + 1) * J], kv[:, x * P:(x + 1) * P], m.ident[0:J, 0:J])
                last.then_inc(mul, 1)
                pe.wait_ge(step, 6)
                pe.wait_ge(loaded, 32)
                for x in range(2):
                    last = nc.tensor.matmul(ps[0:J, 4, 0:D], kvT[:, x, :], wo[:, x, :], start=(x == 0), stop=(x == 1))
                last.then_inc(mul, 1)

        with Stage(nc, "mixo") as s:
            qs, qT = s.sb("qs", [R, U, J]), s.sb("qT", [J + 1, U, R])
            pst, pso = s.ps("pst", 3), s.ps("pso", U)
            staged, turned, moved, full, free, ones_set = [s.sem(n) for n in ("staged", "turned", "moved", "full", "free", "ones_set")]
            block = s.block()

            @block.gpsimd
            def _(pool):
                nc.gpsimd.memset(qT[J:J + 1], 1.0).then_inc(ones_set, 1)
                pool.wait_ge(ones_set, 1)
                with pool.Fori(0, T // U) as i:
                    for k in range(U):
                        t = i * U + k
                        pool.wait_ge(full, t + 1)
                        nc.gpsimd.tensor_copy(qs[:, k, :], cols(QK[:, ds(t, 1), 0:J])).then_inc(staged, 1)

            @block.tensor
            def _(pe):
                pe.sem_inc(full, U)
                pe.wait_ge(ones_set, 1)
                with pe.Fori(0, T // U) as i:
                    for k in range(U):
                        t = i * U + k
                        pe.wait_ge(staged, t + 1)
                        nc.tensor.transpose(pst[0:J, RING3[k], 0:R], qs[:, k, :], m.ident[0:R, 0:R]).then_inc(turned, 1)
                        pe.wait_ge(moved, t + 1)
                        pe.wait_ge(free, t + 1)
                        nc.tensor.matmul(pso[0:R, k, 0:D], qT[:, k, :], KVO[:], start=True, stop=True).then_inc(full, 1)

            @block.scalar
            def _(act):
                with act.Fori(0, T // U) as i:
                    for k in range(U):
                        act.wait_ge(turned, i * U + k + 1)
                        nc.scalar.activation(qT[0:J, k, :], pst[0:J, RING3[k], 0:R], ACT.Copy).then_inc(moved, 1)

            @block.vector
            def _(dve):
                dve.sem_inc(free, U)
                with dve.Fori(0, T // U) as i:
                    for k in range(U):
                        t = i * U + k
                        dve.wait_ge(full, t + 1 + U)
                        xt = cols(XN[:, ds(t, 1), :])
                        nc.vector.tensor_tensor(xt, xt, pso[0:R, k, 0:D], ALU.add).then_inc(free, 1)




def stage_gates(nc, m, name, xT, w, b, E, second_softmax, GATE, b2, X):
    with ExitStack() as c:
        PR = c.enter_context(nc.sbuf_tensor(f"{name}_PR", [R, T, E], F32))[:]
        with Stage(nc, name + "r") as s:
            wt, bt = s.sb("w", [P, 2, E]), s.sb("b", [R, E])
            loaded = s.sem("loaded")
            rp = RowProducts(nc, s, [(xT, 2)], [(E, [wt[:, x, :] for x in range(2)])], 1, lambda pe: pe.wait_ge(loaded, 32))
            block = s.block()

            @block.sync
            def _(sp):
                sp.dma_start(wt[:], w.rearrange("(c p) e -> p c e", p=P)).then_inc(loaded, 16)
                sp.dma_start(bt[:], b.partition_broadcast(R)).then_inc(loaded, 16)

            @block.gpsimd
            def _(pool):
                rp.stage(pool)

            @block.tensor
            def _(pe):
                rp.multiply(pe)

            @block.vector
            def _(dve):
                dve.wait_ge(loaded, 32)
                rp.read(dve, lambda i, k, t: nc.vector.tensor_tensor(cols(PR[:, ds(t, 1), :]), rp.psum(k, 0), bt[:], ALU.add))

        with Stage(nc, name + "g") as s:
            red, cmp, rank = s.sb("red", [R, T]), s.sb("cmp", [R, T, E]), s.sb("rank", [R, T, E])
            step, ex = s.sem("step"), s.sem("ex")
            block = s.block()
            wide = [R, T, E]

            def spread(x):
                return x.unsqueeze(2).to_broadcast(wide)

            @block.vector
            def _(dve):
                drain = nc.vector.drain

                def divide(x):
                    drain()
                    nc.vector.tensor_reduce(red[:], x, AX_X, ALU.add)
                    drain()
                    nc.vector.reciprocal(red[:], red[:])
                    drain()
                    nc.vector.tensor_tensor(x, x, spread(red[:]), ALU.mult)
                    drain()
                nc.vector.tensor_reduce(red[:], PR, AX_X, ALU.max)
                drain()
                nc.vector.tensor_tensor(PR, PR, spread(red[:]), ALU.subtract).then_inc(step, 1)
                dve.wait_ge(ex, 1)
                divide(PR)
                nc.vector.memset(rank[:], 0.0)
                drain()
                for e in range(E):
                    pe_ = PR[:, :, e:e + 1].to_broadcast(wide)
                    nc.vector.tensor_tensor(cmp[:], pe_, PR, ALU.is_gt)
                    drain()
                    nc.vector.tensor_tensor(rank[:], rank[:], cmp[:], ALU.add)
                    drain()
                    if e < E - 1:
                        after = [R, T, E - 1 - e]
                        nc.vector.tensor_tensor(cmp[:, :, e + 1:], PR[:, :, e:e + 1].to_broadcast(after), PR[:, :, e + 1:], ALU.is_equal)
                        drain()
                        nc.vector.tensor_tensor(rank[:, :, e + 1:], rank[:, :, e + 1:], cmp[:, :, e + 1:], ALU.add)
                        drain()
                nc.vector.tensor_scalar(rank[:], rank[:], 2.0, None, ALU.is_lt)
                if second_softmax:
                    nc.vector.tensor_reduce(red[:], PR, AX_X, ALU.max)
                    drain()
                    nc.vector.tensor_tensor(PR, PR, spread(red[:]), ALU.subtract).then_inc(step, 1)
                    dve.wait_ge(ex, 2)
                drain()
                nc.vector.tensor_tensor(PR, PR, rank[:], ALU.mult)
                divide(PR)
                nc.vector.tensor_copy(GATE.rearrange("p e t -> p t e"), PR)

            @block.scalar
            def _(act):
                act.wait_ge(step, 1)
                nc.scalar.activation(PR, PR, ACT.Exp).then_inc(ex, 1)
                if second_softmax:
                    act.wait_ge(step, 2)
                    nc.scalar.activation(PR, PR, ACT.Exp).then_inc(ex, 1)

        with Stage(nc, name + "b") as s:
            bt = s.sb("b", [E, D])
            gs, gT = s.sb("gs", [R, U, E]), s.sb("gT", [E, U, R])
            pst, pso = s.ps("pst", 3), s.ps("pso", U)
            staged, turned, moved, full, free, loaded = [s.sem(n) for n in ("staged", "turned", "moved", "full", "free", "loaded")]
            block = s.block()

            @block.sync
            def _(sp):
                sp.dma_start(bt[:], b2).then_inc(loaded, 16)

            @block.gpsimd
            def _(pool):
                with pool.Fori(0, T // U) as i:
                    for k in range(U):
                        t = i * U + k
                        pool.wait_ge(full, t + 1)
                        nc.gpsimd.tensor_copy(gs[:, k, :], cols(PR[:, ds(t, 1), :])).then_inc(staged, 1)

            @block.tensor
            def _(pe):
                pe.sem_inc(full, U)
                pe.wait_ge(loaded, 16)
                with pe.Fori(0, T // U) as i:
                    for k in range(U):
                        t = i * U + k
                        pe.wait_ge(staged, t + 1)
                        nc.tensor.transpose(pst[0:E, RING3[k], 0:R], gs[:, k, :], m.ident[0:R, 0:R]).then_inc(turned, 1)
                        pe.wait_ge(moved, t + 1)
                        pe.wait_ge(free, t + 1)
                        nc.tensor.matmul(pso[0:R, k, 0:D], gT[:, k, :], bt[:], start=True, stop=True).then_inc(full, 1)

            @block.scalar
            def _(act):
                with act.Fori(0, T // U) as i:
                    for k in range(U):
                        act.wait_ge(turned, i * U + k + 1)
                        nc.scalar.activation(gT[:, k, :], pst[0:E, RING3[k], 0:R], ACT.Copy).then_inc(moved, 1)

            @block.vector
            def _(dve):
                dve.sem_inc(free, U)
                with dve.Fori(0, T // U) as i:
                    for k in range(U):
                        t = i * U + k
                        dve.wait_ge(full, t + 1 + U)
                        xt = cols(X[:, ds(t, 1), :])
                        nc.vector.tensor_tensor(xt, xt, pso[0:R, k, 0:D], ALU.add).then_inc(free, 1)




GROUP = U * R
H0 = (GROUP + 1) // 2
HALVES = [(0, H0), (H0, GROUP - H0)]


def stage_experts(nc, m, name, E, xT, gain_shift, w1, b1, w2, GATE, X):
    HID = 1024
    MH = HID // P
    pairs = max(E // 2, 1)
    pars = range(min(E, 2))
    with Stage(nc, name) as s:
        wa, wb = s.sb("wa", [P, 2, 2, HID]), s.sb("wb", [P, 2, MH, D])
        bt = s.sb("b1", [P, E, MH])
        xe = s.sb("xe", [P, 2, GROUP])
        hT = s.sb("hT", [P, MH, GROUP])
        psh, psy = s.ps("psh", 4), s.ps("psy", 3)
        if gain_shift is not None:
            gb = s.sb("gb", [P, E + 1, 4])
        small_in = s.sem("small_in")
        w_in = [s.sem(f"w_in{p}") for p in range(2)]
        xe_ready, h_full, h_ready, y_full, y_free = [s.sem(n) for n in ("xe_ready", "h_full", "h_ready", "y_full", "y_free")]
        block = s.block()
        nchunks = T // U

        @block.sync
        def _(sp):
            sp.dma_start(bt[:], b1).then_inc(small_in, 16)
            if gain_shift is not None:
                sp.dma_start(gb[:, 0:E], gain_shift).then_inc(small_in, 16)
                sp.dma_start(gb[:, E], gain_shift[:, 0]).then_inc(small_in, 16)
            with sp.Fori(0, pairs) as i:
                for p in pars:
                    e = i * 2 + p
                    wait_apart(sp, s.tick, y_full, (e + 1) * (nchunks * U))
                    sp.dma_start(wa[:, p], w1[ds(e, 1)].rearrange("o (c p) n -> p (o c) n", p=P)).then_inc(w_in[p], 16)
                    sp.dma_start(wb[:, p], w2[ds(e, 1)].rearrange("o (c p) n -> p (o c) n", p=P)).then_inc(w_in[p], 16)

        @block.tensor
        def _(pe):
            pe.sem_inc(y_full, 2 * nchunks * U)
            with pe.Fori(0, pairs) as i:
                for p in pars:
                    wait_apart(pe, s.tick, w_in[p], (i + 1) * 32)
                    with pe.Fori(0, nchunks) as j:
                        n = (i * 2 + p) * nchunks + j
                        if gain_shift is not None:
                            pe.wait_ge(xe_ready, n + 1)
                        for o in range(MH):
                            for hf, (c0, cn) in enumerate(HALVES):
                                job = 2 * o + hf
                                pe.wait_ge(h_ready, n * (2 * MH) + job + 1)
                                for c in range(2):
                                    right = xe[:, c, c0:c0 + cn] if gain_shift is not None else xT[:, c, ds(j * GROUP + c0, cn)]
                                    last = nc.tensor.matmul(psh[:, job % 4, 0:cn], wa[:, p, c, o * P:(o + 1) * P], right,
                                                            start=(c == 0), stop=(c == 1))
                                last.then_inc(h_full, 1)
                        pe.wait_ge(h_ready, (n + 1) * (2 * MH) + 4)
                        for k in range(U):
                            pe.wait_ge(y_free, n * U + k + 1)
                            for c in range(MH):
                                last = nc.tensor.matmul(psy[0:R, RING3[k], 0:D], hT[:, c, k * R:(k + 1) * R],
                                                        wb[:, p, c, :], start=(c == 0), stop=(c == MH - 1))
                            last.then_inc(y_full, 1)

        @block.scalar
        def _(act):
            act.sem_inc(h_ready, 4)
            act.wait_ge(small_in, 48 if gain_shift is not None else 16)

            def prepare(e, j):
                if gain_shift is None:
                    return
                for c in range(2):
                    gain = gb[:, ds(e, 1), c:c + 1].rearrange("p a b -> p (a b)")
                    shift = gb[:, ds(e, 1), 2 + c:3 + c].rearrange("p a b -> p (a b)")
                    last = nc.scalar.activation(xe[:, c, :], xT[:, c, ds(j * GROUP, GROUP)], ACT.Identity, bias=shift, scale=gain)
                last.then_inc(xe_ready, 1)

            def hidden(e, j):
                n = e * nchunks + j
                act.wait_ge(y_full, (n + 2 * nchunks) * U)
                for o in range(MH):
                    for hf, (c0, cn) in enumerate(HALVES):
                        wait_apart(act, s.tick, h_full, n * (2 * MH) + 2 * o + hf + 1)
                        nc.scalar.activation(hT[:, o, c0:c0 + cn], psh[:, (2 * o + hf) % 4, 0:cn], ACT.Gelu,
                                             bias=bt[:, ds(e, 1), o:o + 1].rearrange("p a b -> p (a b)")).then_inc(h_ready, 1)
            prepare(0, 0)
            with act.Fori(0, pairs) as i:
                for p in pars:
                    e = i * 2 + p
                    with act.Fori(0, nchunks - 1) as j:
                        hidden(e, j)
                        prepare(e, j + 1)
                    hidden(e, nchunks - 1)
                    prepare(e + 1, 0)

        @block.vector
        def _(dve):
            dve.sem_inc(y_free, 2)
            with dve.Fori(0, pairs) as i:
                for p in pars:
                    with dve.Fori(0, nchunks) as j:
                        e = i * 2 + p
                        n = e * nchunks + j
                        for k in range(U):
                            dve.wait_ge(y_full, (n + 2 * nchunks) * U + k + 1)
                            xt = cols(X[:, ds(j * U + k, 1), :])
                            y = psy[0:R, RING3[k], 0:D]
                            if GATE is None:
                                nc.vector.tensor_tensor(xt, xt, y, ALU.add).then_inc(y_free, 1)
                            else:
                                gate = GATE[:, ds(e, 1), ds(j * U + k, 1)].rearrange("p a b -> p (a b)")
                                nc.vector.scalar_tensor_tensor(out=xt, in0=y, scalar=gate, in1=xt, op0=ALU.mult, op1=ALU.add).then_inc(y_free, 1)
                        nc.vector.drain()




def stage_linear_attention(nc, m, a, xT, WEFF):
    HEADS, DH = 8, 64
    IN = HEADS * DH
    PAIRS = IN // P
    with ExitStack() as cc:
        DOTS = cc.enter_context(nc.sbuf_tensor("lin_DOTS", [P, PAIRS, P], F32))[:]
        with Stage(nc, "lina") as s:
            wkv = s.sb("wkv", [P, 2, 2 * IN])
            xs = s.sb("xs", [P, U, 2, R])
            kv = s.sb("kv", [R, 3, 2, IN])
            sq = s.sb("sq", [R, 2 * IN])
            mu, var, std, eps = s.sb("mu", [R, 16]), s.sb("var", [R, 16]), s.sb("std", [R, 16]), s.sb("eps", [R, 1])
            ps, psd = s.ps("ps", 6), s.ps("psd", 1)
            loaded, staged, full, free, centred, squared, var_ready, std_ready, normed, dotted = [
                s.sem(n) for n in ("loaded", "staged", "full", "free", "centred", "squared", "var_ready", "std_ready", "normed", "dotted")]
            block = s.block()

            @block.sync
            def _(sp):
                sp.dma_start(wkv[:], a["w_kvT"].rearrange("(c p) n -> p c n", p=P)).then_inc(loaded, 16)

            @block.gpsimd
            def _(pool):
                with pool.Fori(0, T // U) as i:
                    for k in range(U):
                        t = i * U + k
                        pool.wait_ge(full, t + 1)
                        nc.gpsimd.tensor_copy(xs[:, k], xT[:, :, ds(t * R, R)]).then_inc(staged, 1)

            @block.tensor
            def _(pe):
                pe.sem_inc(full, U)
                pe.wait_ge(loaded, 16)

                def project(t, k):
                    pe.wait_ge(staged, t + 1)
                    pe.wait_ge(free, t + 1)
                    for j in range(2):
                        for c in range(2):
                            last = nc.tensor.matmul(ps[0:R, 2 * RING3[k] + j, 0:IN], xs[:, k, c, :], wkv[:, c, j * IN:(j + 1) * IN],
                                                    start=(c == 0), stop=(c == 1))
                    last.then_inc(full, 1)

                def dots(t, k, first, last_tile):
                    pe.wait_ge(normed, t + 1)
                    for x in range(PAIRS):
                        last = nc.tensor.matmul(psd[:, 0, x * P:(x + 1) * P], kv[:, RING3[k], 1, x * P:(x + 1) * P], kv[:, RING3[k], 0, x * P:(x + 1) * P],
                                                start=first and x == 0, stop=last_tile, skip_group_check=True)
                    last.then_inc(dotted, 1)
                project(0, 0)
                for k in range(U):
                    project(k + 1, (k + 1) % U)
                    dots(k, k, k == 0, False)
                with pe.Fori(1, T // U - 1) as i:
                    for k in range(U):
                        project(i * U + k + 1, (k + 1) % U)
                        dots(i * U + k, k, False, False)
                for k in range(U):
                    t = T - U + k
                    if k < U - 1:
                        project(t + 1, k + 1)
                    dots(t, k, False, k == U - 1)

            @block.vector
            def _(dve):
                dve.sem_inc(free, 2)
                nc.vector.memset(eps[:], EPS)
                heads = "p j (h f) -> p (j h) f"
                with dve.Fori(0, T // U) as i:
                    for k in range(U):
                        t = i * U + k
                        dve.wait_ge(full, t + 1 + U)
                        x = ps[0:R, 2 * RING3[k]:2 * RING3[k] + 2, 0:IN].rearrange(heads, f=DH)
                        y = kv[:, RING3[k]].rearrange(heads, f=DH)
                        nc.vector.tensor_reduce(mu[:], x, AX_X, ALU.add)
                        nc.vector.drain()
                        nc.vector.tensor_scalar(mu[:], mu[:], 1.0 / DH, None, ALU.mult)
                        nc.vector.drain()
                        dve.wait_ge(dotted, t + 1)
                        nc.vector.tensor_tensor(y, x, mu[:].unsqueeze(2).to_broadcast([R, 16, DH]), ALU.subtract).then_inc(centred, 1)
                        nc.vector.drain().then_inc(free, 1)
                        dve.wait_ge(squared, t + 1)
                        nc.vector.tensor_reduce(var[:], sq[:].rearrange("p (h f) -> p h f", f=DH), AX_X, ALU.add).then_inc(var_ready, 1)
                        dve.wait_ge(std_ready, t + 1)
                        nc.vector.reciprocal(std[:], std[:])
                        nc.vector.drain()
                        nc.vector.tensor_tensor(y, y, std[:].unsqueeze(2).to_broadcast([R, 16, DH]), ALU.mult).then_inc(normed, 1)
                dve.wait_ge(dotted, T + 2)
                for x in range(PAIRS):
                    nc.vector.scalar_tensor_tensor(out=DOTS[:, x, :], in0=psd[:, 0, x * P:(x + 1) * P], scalar=1.0 / N, in1=m.pairmask, op0=ALU.mult, op1=ALU.mult)

            @block.scalar
            def _(act):
                act.sem_inc(dotted, 2)
                with act.Fori(0, T // U) as i:
                    for k in range(U):
                        t = i * U + k
                        act.wait_ge(centred, t + 1)
                        nc.scalar.activation(sq[:], kv[:, RING3[k]].rearrange("p j n -> p (j n)"), ACT.Square).then_inc(squared, 1)
                        act.wait_ge(var_ready, t + 1)
                        nc.scalar.activation(std[:], var[:], ACT.Sqrt, bias=eps[:, 0:1], scale=1.0 / DH).then_inc(std_ready, 1)

        with Stage(nc, "linb") as s:
            wq, wo = s.sb("wq", [P, PAIRS, D]), s.sb("wo", [P, PAIRS, D])
            mo = s.sb("mo", [P, PAIRS, D])
            ps, psw = s.ps("ps", PAIRS), s.ps("psw", 2)
            loaded, full, moved, done = s.sem("loaded"), s.sem("full"), s.sem("moved"), s.sem("done")
            block = s.block()

            @block.sync
            def _(sp):
                sp.dma_start(wq[:], a["w_q"].rearrange("(c p) n -> p c n", p=P)).then_inc(loaded, 16)
                sp.dma_start(wo[:], a["w_outT"].rearrange("(c p) n -> p c n", p=P)).then_inc(loaded, 16)

            @block.tensor
            def _(pe):
                pe.wait_ge(loaded, 32)
                for x in range(PAIRS):
                    nc.tensor.matmul(ps[:, x, 0:D], DOTS[:, x, :], wo[:, x, :], start=True, stop=True).then_inc(full, 1)
                pe.wait_ge(moved, PAIRS)
                for c in range(2):
                    for x in range(PAIRS):
                        last = nc.tensor.matmul(psw[:, c, 0:D], wq[:, x, c * P:(c + 1) * P], mo[:, x, :], start=(x == 0), stop=(x == PAIRS - 1))
                last.then_inc(done, 1)

            @block.scalar
            def _(act):
                for x in range(PAIRS):
                    act.wait_ge(full, x + 1)
                    nc.scalar.activation(mo[:, x, :], ps[:, x, 0:D], ACT.Copy).then_inc(moved, 1)
                act.wait_ge(done, 1)
                nc.scalar.activation(WEFF, psw[:, :, 0:D], ACT.Copy)


def stage_rows_add(nc, m, name, parts, X):
    with Stage(nc, name) as s:
        loaded = s.sem("loaded")
        rhs, loads = [], []
        for j, (xT, c, w) in enumerate(parts):
            if w.shape[0] == c * P:
                wt = s.sb(f"w{j}", [P, c, D])
                loads.append((wt, w))
                w = wt[:]
            rhs += [w[:, x, :] for x in range(c)]
        rp = RowProducts(nc, s, [(xT, c) for xT, c, _ in parts], [(D, rhs)], 1, lambda pe: pe.wait_ge(loaded, 16 * len(loads)))
        block = s.block()

        @block.sync
        def _(sp):
            for wt, w in loads:
                sp.dma_start(wt[:], w.rearrange("(c p) n -> p c n", p=P)).then_inc(loaded, 16)

        @block.gpsimd
        def _(pool):
            rp.stage(pool)

        @block.tensor
        def _(pe):
            rp.multiply(pe)

        @block.vector
        def _(dve):
            def add(i, k, t):
                xt = cols(X[:, ds(t, 1), :])
                return nc.vector.tensor_tensor(xt, xt, rp.psum(k, 0), ALU.add)
            rp.read(dve, add)




def stage_last_ffn(nc, m, a, xT, GATE, X):
    E = 4
    with Stage(nc, "ffn") as s:
        w1, w2, w3 = s.sb("w1", [P, 2, 2 * P]), s.sb("w2", [P, 2, P]), s.sb("w3", [P, D])
        e1, e2, e3 = s.sb("e1", [P, E, 2, P]), s.sb("e2", [P, E, 64]), s.sb("e3", [64, E, D])
        b1, b2, c1, c2 = s.sb("b1", [P, 2]), s.sb("b2", [P, 1]), s.sb("c1", [P, E]), s.sb("c2", [64, E])
        h1, h2 = s.sb("h1", [P, 2, GROUP]), s.sb("h2", [P, GROUP])
        g1, g2 = s.sb("g1", [P, E, GROUP]), s.sb("g2", [64, E, GROUP])
        psh, psy = s.ps("psh", 4), s.ps("psy", 3)
        loaded, h_full, h_ready, y_full, y_free = [s.sem(n) for n in ("loaded", "h_full", "h_ready", "y_full", "y_free")]
        block = s.block()
        cut = lambda t: (lambda c0, cn: t[:, c0:c0 + cn])
        layers = []
        xin = [("x", c) for c in range(2)]
        for o in range(2):
            layers.append((P, [w1[:, c, o * P:(o + 1) * P] for c in range(2)], xin, h1[:, o, :], b1[:, o:o + 1], 0))
        for e in range(E):
            layers.append((P, [e1[:, e, c, :] for c in range(2)], xin, g1[:, e, :], c1[:, e:e + 1], 0))
        layers.append((P, [w2[:, c, :] for c in range(2)], [h1[:, 0, :], h1[:, 1, :]], h2[:], b2[:, 0:1], 2))
        for e in range(E):
            layers.append((64, [e2[:, e, :]], [g1[:, e, :]], g2[:, e, :], c2[:, e:e + 1], 3 + e))
        JOBS_ = 2 * len(layers)
        outs = [(h2, w3[:], None)] + [(g2[:, e, :], e3[:, e, :], e) for e in range(E)]
        YS = U * len(outs)
        SLOTS = 2

        @block.sync
        def _(sp):
            pairs = [(w1[:], a["L1_ffn_sW1"].rearrange("(c p) n -> p c n", p=P)), (w2[:], a["L1_ffn_sW2"].rearrange("(c p) n -> p c n", p=P)),
                     (w3[:], a["L1_ffn_sW3"]), (e2[:], a["L1_ffn_eW2"].rearrange("e p n -> p e n")), (e3[:], a["L1_ffn_eW3"].rearrange("e p n -> p e n")),
                     (b1[:], a["c_sb1"]), (b2[:], a["c_sb2"]), (c1[:], a["c_eb1"]), (c2[:], a["c_eb2"])]
            pairs += [(e1[:, e], a["L1_ffn_eW1"][e].rearrange("(c p) n -> p c n", p=P)) for e in range(E)]
            for dst, src in pairs:
                sp.dma_start(dst, src).then_inc(loaded, 16)

        LOADS = 9 + E

        @block.tensor
        def _(pe):
            pe.wait_ge(loaded, 16 * LOADS)
            with pe.Fori(0, T // U) as j:
                for o, (rows, left, right, _, _, need) in enumerate(layers):
                    for hf, (c0, cn) in enumerate(HALVES):
                        job = 2 * o + hf
                        pe.wait_ge(h_ready, j * JOBS_ + max(job + 1, 2 * need + 4 if need else 0))
                        for c, lhs in enumerate(left):
                            x = right[c]
                            x = xT[:, x[1], ds(j * GROUP + c0, cn)] if isinstance(x, tuple) else x[:, c0:c0 + cn]
                            last = nc.tensor.matmul(psh[0:rows, job % 4, 0:cn], lhs, x, start=(c == 0), stop=(c == len(left) - 1))
                        last.then_inc(h_full, 1)
                pe.wait_ge(h_ready, (j + 1) * JOBS_ + 4)
                for k in range(U):
                    for y, (src, right, _) in enumerate(outs):
                        pe.wait_ge(y_free, j * YS + k * len(outs) + y + 1)
                        nc.tensor.matmul(psy[0:R, RING3[y], 0:D], src[:, k * R:(k + 1) * R], right,
                                         start=True, stop=True).then_inc(y_full, 1)

        @block.scalar
        def _(act):
            act.sem_inc(h_ready, 4)
            act.sem_inc(y_full, YS)
            act.wait_ge(loaded, 16 * LOADS)
            with act.Fori(0, T // U) as j:
                act.wait_ge(y_full, (j + 1) * YS)
                for o, (rows, _, _, dst, bias, _) in enumerate(layers):
                    for hf, (c0, cn) in enumerate(HALVES):
                        job = 2 * o + hf
                        act.wait_ge(h_full, j * JOBS_ + job + 1)
                        nc.scalar.activation(dst[:, c0:c0 + cn], psh[0:rows, job % 4, 0:cn], ACT.Relu, bias=bias).then_inc(h_ready, 1)

        @block.vector
        def _(dve):
            dve.sem_inc(y_free, SLOTS)
            with dve.Fori(0, T // U) as j:
                for k in range(U):
                    for y, (_, _, e) in enumerate(outs):
                        dve.wait_ge(y_full, (j + 1) * YS + k * len(outs) + y + 1)
                        xt = cols(X[:, ds(j * U + k, 1), :])
                        ps = psy[0:R, RING3[y], 0:D]
                        if e is None:
                            nc.vector.tensor_tensor(xt, xt, ps, ALU.add).then_inc(y_free, 1)
                        else:
                            gate = GATE[:, e:e + 1, ds(j * U + k, 1)].rearrange("p a b -> p (a b)")
                            nc.vector.scalar_tensor_tensor(out=xt, in0=ps, scalar=gate, in1=xt, op0=ALU.mult, op1=ALU.add).then_inc(y_free, 1)
                        nc.vector.drain()




class Machine:
    pass


def build(nc, a, out):
    m = Machine()
    m.src, m.dst = a["src"], a["dst"]

    def dram(name, shape, dt=F32):
        return nc.dram_tensor(name, shape, dt).ap()
    m.QB = dram("edge_codes", [EDGES + CAP, 2])
    m.LO = dram("window_starts", [25, 25], I32)
    m.CT = dram("counts", [N, N])
    m.MK = dram("mask", [N * T, R], BF16)
    m.ALS = dram("source_scores", [4 * T, R])
    m.UV = dram("target_terms", [2, 4 * T, R])
    with ExitStack() as ctx:
        def sb(name, shape, dt=F32, c=ctx):
            return c.enter_context(nc.sbuf_tensor(name, shape, dt))
        nconst = a["consts"].shape[1]
        C = sb("C", [P, nconst])
        m.flag = sb("flag", [1, 1], I32)
        at = [0]

        def take(n):
            at[0] += n
            return C[:, at[0] - n:at[0]]
        m.ident, m.iota, m.below, m.ones = take(P), take(P), take(P), take(P)
        m.headmask, m.pairmask, m.wstart, m.pcol = take(D), take(P), take(NW), take(1)
        X = sb("X", [R, T, D])[:]
        MEAN, RSTD = sb("MEAN", [R, T])[:], sb("RSTD", [R, T])[:]
        x_rows = a["x"].rearrange("(t p) d -> p t d", p=R)
        with Stage(nc, "load") as s:
            loaded = s.sem("loaded")
            block = s.block()

            @block.sync
            def _(sp):
                sp.dma_start(C[:], a["consts"]).then_inc(loaded, 16)
                tile_dma(sp, X, x_rows, loaded)
                sp.wait_ge(loaded, 48)

        stage_edge_codes(nc, m)
        with ExitStack() as c:
            K = sb("K", [P, 4, NW], F32, c)[:]
            stage_keys(nc, m, K)
            stage_counts(nc, m, K)
        stage_counts_general(nc, m)

        g0 = Gat(nc, "g0", 4, 64, 4, "relu")
        with ExitStack() as c:
            AL = sb("g0_AL", [R, 2 * 4, T], F32, c)[:]
            with ExitStack() as c1:
                XN, XT, XM = sb("XN0", [R, T, D], F32, c1)[:], sb("XT0", [P, 2, N], F32, c1)[:], sb("XM0", [P, 2, N], F32, c1)[:]
                stage_stats(nc, "st0", X, MEAN, RSTD)
                stage_norm(nc, m, "nm0", X, MEAN, RSTD, XT, out_rows=XN)
                stage_gat_project(nc, m, g0, XT, 2, a["L0_gnn_W"], a["L0_gnn_att_src"], a["L0_gnn_att_dst"], AL)
                stage_stats(nc, "st1", XN, MEAN, RSTD)
                stage_norm(nc, m, "nm1", XN, MEAN, RSTD, XT, affine=a["c_ln1"])
                stage_linear(nc, "xm", XT, 2, a["L0_mix_Wx"], a["c_bx"], 2, ACT.Identity, XM)
                stage_mix(nc, m, a, XM, XN)
                stage_stats(nc, "st2", XN, MEAN, RSTD)
                stage_norm(nc, m, "nm2", XN, MEAN, RSTD, XT, affine=a["c_ln2"])
                stage_add_row(nc, "ar0", [a["L0_mix_b2"]], X, more=XN)
                stage_experts(nc, m, "mlp", 1, XT, None, a["L0_mix_W1"].unsqueeze(0), a["c_mlp_b1"], a["L0_mix_W2"].unsqueeze(0), None, X)
            GT = sb("GT0", [64, 4, N], F32, c)[:]
            graph_attention(nc, m, g0, AL, a["c_g0_bias"], GT)
            stage_add_transposed(nc, m, "at0", GT, 64, 4, X)

        with ExitStack() as c:
            GATE = sb("GATE0", [R, 8, T], F32, c)[:]
            XT = sb("XT1", [P, 2, N], F32, c)[:]
            with ExitStack() as c1:
                XN = sb("XN1", [R, T, D], F32, c1)[:]
                stage_stats(nc, "st3", X, MEAN, RSTD)
                stage_norm(nc, m, "nm3", X, MEAN, RSTD, XT, out_rows=XN)
                stage_gates(nc, m, "gt0", XT, a["L0_ffn_Wr"], a["L0_ffn_br"], 8, False, GATE, a["L0_ffn_b2"], X)
                stage_stats(nc, "st4", XN, MEAN, RSTD)
                stage_norm(nc, m, "nm4", XN, MEAN, RSTD, XT)
            stage_experts(nc, m, "moe", 8, XT, a["c_moe_ln"], a["L0_ffn_W1"], a["c_moe_b1"], a["L0_ffn_W2"], GATE, X)

        g1, g2, g3 = Gat(nc, "g1", 4, P, 2, "elu"), Gat(nc, "g2", 4, P, 2, "elu"), Gat(nc, "g3", 1, D, 1, "plain")
        with ExitStack() as c:
            XT, GT = sb("XT2", [P, 2, N], F32, c)[:], sb("GT1", [P, 4, N], F32, c)[:]
            stage_stats(nc, "st5", X, MEAN, RSTD)
            stage_norm(nc, m, "nm5", X, MEAN, RSTD, XT)
            for g, src, KC, dst, n in ((g1, XT, 2, GT, 1), (g2, GT, 4, GT, 2), (g3, GT, 4, GT[:, 0:2], 3)):
                with ExitStack() as c1:
                    AL = sb(f"{g.name}_AL", [R, 2 * g.heads, T], F32, c1)[:]
                    stage_gat_project(nc, m, g, src, KC, a[f"L1_gnn_W{n}"], a[f"L1_gnn_a_src{n}"], a[f"L1_gnn_a_dst{n}"], AL)
                    graph_attention(nc, m, g, AL, a[f"c_{g.name}_bias"], dst)
            stage_linear(nc, "m1", GT[:, 0:2], 2, a["L1_gnn_M1"], a["c_mb1"], 2, ACT.Relu, GT[:, 2:4])
            stage_linear(nc, "m2", GT[:, 2:4], 2, a["L1_gnn_M2"], a["c_mb2"], 1, ACT.Relu, GT[:, 0:1])
            WEFF = sb("WEFF", [P, 2, D], F32, c)[:]
            stage_linear_attention(nc, m, a, XT, WEFF)
            stage_rows_add(nc, m, "m3", [(GT[:, 0:1], 1, a["L1_gnn_M3"]), (XT, 2, WEFF)], X)
            stage_add_row(nc, "ar1", [a["L1_gnn_mb3"], a["L1_mix_b_out"]], X)

        with ExitStack() as c:
            XT, GATE = sb("XT3", [P, 2, N], F32, c)[:], sb("GATE1", [R, 4, T], F32, c)[:]
            stage_stats(nc, "st6", X, MEAN, RSTD)
            stage_norm(nc, m, "nm6", X, MEAN, RSTD, XT)
            stage_gates(nc, m, "gt1", XT, a["L1_ffn_gW"], a["L1_ffn_gb"], 4, True, GATE, a["L1_ffn_eb3"], X)
            stage_add_row(nc, "ar2", [a["L1_ffn_sb3"]], X)
            stage_last_ffn(nc, m, a, XT, GATE, X)

        with Stage(nc, "store") as s:
            stored = s.sem("stored")
            block = s.block()

            @block.sync
            def _(sp):
                tile_dma(sp, out.rearrange("(t p) d -> p t d", p=R), X, stored)
                sp.wait_ge(stored, 32)




def laid_out(v):
    import numpy as np

    g = {k: np.asarray(x) for k, x in v.items()}

    def columns(x, p=P):
        x = x.reshape(*x.shape[:-1], -1, p)
        return np.moveaxis(x, -1, 0)

    as_is = ["x", "src", "dst", "L0_gnn_W", "L0_gnn_att_src", "L0_gnn_att_dst", "L0_mix_Wx", "L0_mix_Wq", "L0_mix_Wk", "L0_mix_Wv",
             "L0_mix_Wo", "L0_mix_bo", "L0_mix_W1", "L0_mix_W2", "L0_mix_b2", "L0_ffn_Wr", "L0_ffn_br", "L0_ffn_W1", "L0_ffn_W2",
             "L0_ffn_b2", "L1_gnn_W1", "L1_gnn_a_src1", "L1_gnn_a_dst1", "L1_gnn_W2", "L1_gnn_a_src2", "L1_gnn_a_dst2", "L1_gnn_W3",
             "L1_gnn_a_src3", "L1_gnn_a_dst3", "L1_gnn_M1", "L1_gnn_M2", "L1_gnn_M3", "L1_gnn_mb3", "L1_mix_b_out", "L1_ffn_sW1",
             "L1_ffn_sW2", "L1_ffn_sW3", "L1_ffn_sb3", "L1_ffn_eW1", "L1_ffn_eW2", "L1_ffn_eW3", "L1_ffn_eb3", "L1_ffn_gW", "L1_ffn_gb"]
    r = {k: g[k] for k in as_is}
    qkv = g["L1_mix_w_qkv"]
    inner = qkv.shape[0] // 3
    r["w_q"], r["w_kvT"], r["w_outT"] = qkv[:inner], qkv[inner:].T, g["L1_mix_w_out"].T
    r["c_ln1"] = np.concatenate([columns(g["L0_mix_ln1_g"]), columns(g["L0_mix_ln1_b"])], 1)
    r["c_ln2"] = np.concatenate([columns(g["L0_mix_ln2_g"]), columns(g["L0_mix_ln2_b"])], 1)
    r["c_moe_ln"] = np.concatenate([columns(g["L0_ffn_ln_g"]), columns(g["L0_ffn_ln_b"])], 2)
    r["c_bx"], r["c_mlp_b1"], r["c_moe_b1"] = columns(g["L0_mix_bx"]), columns(g["L0_mix_b1"][None]), columns(g["L0_ffn_b1"])
    r["c_g0_bias"] = columns(g["L0_gnn_bias"], 64)
    for n in (1, 2, 3):
        r[f"c_g{n}_bias"] = columns(g[f"L1_gnn_b{n}"])
    r["c_mb1"], r["c_mb2"] = columns(g["L1_gnn_mb1"]), columns(g["L1_gnn_mb2"])
    r["c_sb1"], r["c_sb2"] = columns(g["L1_ffn_sb1"]), columns(g["L1_ffn_sb2"])
    r["c_eb1"], r["c_eb2"] = g["L1_ffn_eb1"].T, g["L1_ffn_eb2"].T
    p, q = np.arange(P)[:, None], np.arange(P)[None, :]
    d = np.arange(D)[None, :]
    r["consts"] = np.concatenate([p == q, q + 0 * p, p < q, 1 + 0 * (p + q), p // 4 == d // 32, p // 64 == q // 64,
                                  QW * np.arange(NW)[None, :] + 0 * p, QW * p], 1).astype(np.float32)
    return {k: np.ascontiguousarray(x) for k, x in r.items()}


def kernel(**inputs):
    import concourse.bacc as bacc
    from concourse.bass_utils import run_bass_kernel_spmd

    arrays = laid_out(inputs)
    nc = bacc.Bacc("TRN2", target_bir_lowering=False, num_devices=1)
    args = {k: nc.dram_tensor(f"in_{k}", list(x.shape), mybir.dt.from_np(x.dtype), kind="ExternalInput").ap() for k, x in arrays.items()}
    out = nc.dram_tensor("out", [N, D], F32, kind="ExternalOutput").ap()
    build(nc, args, out)
    result = run_bass_kernel_spmd(nc, [{f"in_{k}": x for k, x in arrays.items()}], core_ids=[0])
    return result.results[0]["out"]
```
